# Optimizing a Trainium2 kernel written in Bass

```python
import numpy as np
import jax
import jax.numpy as jnp

def _softmax(x, axis=-1):
    return jax.nn.softmax(x, axis=axis)

def _gelu(x):
    return jax.nn.gelu(x, approximate=True)

def _silu(x):
    return jax.nn.silu(x)

def _sigmoid(x):
    return jax.nn.sigmoid(x)

def _layernorm(x, axis=-1, eps=1e-05):
    m = jnp.mean(x, axis=axis, keepdims=True)
    v = jnp.var(x, axis=axis, keepdims=True)
    return (x - m) / jnp.sqrt(v + eps)

def _scatter_add(tgt, idx, src, axis=0):
    return tgt.at[idx].add(src)

def _segment_sum(src, seg, n):
    return jax.ops.segment_sum(src, seg, n)
kernel_name = 'mk_adj_preln_d4_adj_r2_ebcba3'

def setup_inputs(seed: int=0):
    np.random.seed(seed)
    _w = jnp.asarray

    def _rec_inputs():
        import jax
        import jax.numpy as jnp
        _gk = jax.random.key(seed)
        x = -0.0002928 + 1 * jax.random.normal(jax.random.fold_in(_gk, 1), (64, 128, 128), jnp.float32)
        _w = (1.0 + jnp.arange(128, dtype=jnp.float32)) ** (-0.5)
        _w = _w / _w.mean()
        _pij = jnp.clip(0.125 * _w[:, None] * _w[None, :], 0.0, 1.0)
        _a = jax.random.uniform(jax.random.fold_in(_gk, 2), (64, 128, 128)) < _pij
        _a = jnp.logical_or(_a, jnp.swapaxes(_a, -1, -2))
        _a = jnp.logical_or(_a, jnp.eye(128, dtype=bool))
        _af = _a.astype(jnp.float32)
        _af = _af * jax.random.uniform(jax.random.fold_in(_gk, 3), (64, 128, 128), jnp.float32, 0.05, 1)
        adj = _af
        _nm = jnp.ones((64, 128), dtype=bool)
        nodemask = _nm
        return (x, adj, nodemask)
    x, adj, nodemask = _rec_inputs()

    def _L0_gnn_setup():
        import jax, jax.numpy as jnp
        import numpy as np
        NFEAT, NHID = (128, 128)
        key = jax.random.key(seed)
        k1, k2, k3, k4 = jax.random.split(key, 4)
        x = jax.random.normal(k1, (32, 512, NFEAT), dtype=jnp.float32)
        adj = jax.random.uniform(k2, (32, 512, 512), dtype=jnp.float32)
        bound = 1.0 / np.sqrt(NHID)
        W = jax.random.uniform(k3, (NFEAT, NHID), dtype=jnp.float32, minval=-bound, maxval=bound)
        b = jax.random.uniform(k4, (NHID,), dtype=jnp.float32, minval=-bound, maxval=bound)
        return {'x': x, 'adj': adj, 'W': W, 'b': b}
    _L0_gnn_all = _L0_gnn_setup()
    _L0_gnn_in = {k: v for k, v in _L0_gnn_all.items() if k in ('W', 'b')}
    del _L0_gnn_all

    def _L1_gnn_setup():
        import jax, jax.numpy as jnp
        import numpy as np
        B, S, H, HID = (1, 512, 128, 128)
        LN_EPS = 1e-05

        def _layernorm(y, gamma, beta):
            mu = jnp.mean(y, axis=-1, keepdims=True)
            var = jnp.mean(jnp.square(y - mu), axis=-1, keepdims=True)
            return (y - mu) * jax.lax.rsqrt(var + LN_EPS) * gamma + beta
        key = jax.random.key(seed)
        ks = jax.random.split(key, 8)
        x = jax.random.normal(ks[0], (B, S, H), dtype=jnp.float32)
        adj = jax.random.uniform(ks[1], (B, S, S), dtype=jnp.float32)
        W1 = jax.random.normal(ks[2], (2 * H, HID), dtype=jnp.float32) / np.sqrt(2 * H)
        b1 = jnp.zeros((HID,), dtype=jnp.float32)
        W2 = jax.random.normal(ks[3], (HID, HID), dtype=jnp.float32) / np.sqrt(HID)
        b2 = jnp.zeros((HID,), dtype=jnp.float32)
        gamma = jnp.ones((HID,), dtype=jnp.float32)
        beta = jnp.zeros((HID,), dtype=jnp.float32)
        return {'x': x, 'adj': adj, 'W1': W1, 'b1': b1, 'W2': W2, 'b2': b2, 'gamma': gamma, 'beta': beta}
    _L1_gnn_all = _L1_gnn_setup()
    _L1_gnn_in = {k: v for k, v in _L1_gnn_all.items() if k in ('W1', 'b1', 'W2', 'b2', 'gamma', 'beta')}
    del _L1_gnn_all

    def _L2_gnn_setup():
        import jax, jax.numpy as jnp
        import numpy as np
        BS, N, D_IN, D_OUT = (8, 1024, 128, 128)
        key = jax.random.key(seed)
        k1, k2, k3, k4 = jax.random.split(key, 4)
        x = jax.random.normal(k1, (BS, N, D_IN), dtype=jnp.float32)
        adj = jax.random.uniform(k2, (BS, N, N), dtype=jnp.float32)
        theta = jax.random.normal(k3, (D_IN, D_OUT), dtype=jnp.float32) * (1.0 / np.sqrt(D_OUT))
        bias = jax.random.normal(k4, (D_OUT,), dtype=jnp.float32) * (1.0 / np.sqrt(D_OUT))
        return {'x': x, 'adj': adj, 'theta': theta, 'bias': bias}
    _L2_gnn_all = _L2_gnn_setup()
    _L2_gnn_in = {k: v for k, v in _L2_gnn_all.items() if k in ('theta', 'bias')}
    del _L2_gnn_all

    def _L3_gnn_setup():
        import jax, jax.numpy as jnp
        import numpy as np
        B, N, F, H = (16, 512, 128, 128)
        key = jax.random.key(seed)
        k1, k2, k3, k4, k5 = jax.random.split(key, 5)
        x = jax.random.normal(k1, (B, N, F), dtype=jnp.float32)
        adjacency = (jax.random.uniform(k2, (B, N, N)) < 0.05).astype(jnp.float32)
        node_mask = jax.random.uniform(k3, (B, N)) < 0.9
        W1 = jax.random.normal(k4, (F, H), dtype=jnp.float32) / np.sqrt(F)
        b1 = jnp.zeros((H,), dtype=jnp.float32)
        W2 = jax.random.normal(k5, (H, F), dtype=jnp.float32) / np.sqrt(H)
        b2 = jnp.zeros((F,), dtype=jnp.float32)
        eps = jnp.zeros((1,), dtype=jnp.float32)
        return {'x': x, 'adjacency': adjacency, 'node_mask': node_mask, 'W1': W1, 'b1': b1, 'W2': W2, 'b2': b2, 'eps': eps}
    _L3_gnn_all = _L3_gnn_setup()
    _L3_gnn_in = {k: v for k, v in _L3_gnn_all.items() if k in ('W1', 'b1', 'W2', 'b2', 'eps')}
    del _L3_gnn_all
    return {'x': x, 'adj': adj, 'nodemask': nodemask, 'L0_gnn_W': _L0_gnn_in['W'], 'L0_gnn_b': _L0_gnn_in['b'], 'L1_gnn_W1': _L1_gnn_in['W1'], 'L1_gnn_b1': _L1_gnn_in['b1'], 'L1_gnn_W2': _L1_gnn_in['W2'], 'L1_gnn_b2': _L1_gnn_in['b2'], 'L1_gnn_gamma': _L1_gnn_in['gamma'], 'L1_gnn_beta': _L1_gnn_in['beta'], 'L2_gnn_theta': _L2_gnn_in['theta'], 'L2_gnn_bias': _L2_gnn_in['bias'], 'L3_gnn_W1': _L3_gnn_in['W1'], 'L3_gnn_b1': _L3_gnn_in['b1'], 'L3_gnn_W2': _L3_gnn_in['W2'], 'L3_gnn_b2': _L3_gnn_in['b2'], 'L3_gnn_eps': _L3_gnn_in['eps']}

def reference(x, adj, nodemask, L0_gnn_W, L0_gnn_b, L1_gnn_W1, L1_gnn_b1, L1_gnn_W2, L1_gnn_b2, L1_gnn_gamma, L1_gnn_beta, L2_gnn_theta, L2_gnn_bias, L3_gnn_W1, L3_gnn_b1, L3_gnn_W2, L3_gnn_b2, L3_gnn_eps):
    import jax
    import jax.numpy as jnp

    def _L0_gnn_ref(x, adj, W, b):
        import jax, jax.numpy as jnp
        import numpy as np
        NFEAT, NHID = (128, 128)
        support = jnp.einsum('bnf,fh->bnh', x, W)
        out = jnp.einsum('bnm,bmh->bnh', adj, support) + b
        return jax.nn.relu(out)

    def _L1_gnn_ref(x, adj, W1, b1, W2, b2, gamma, beta):
        import jax, jax.numpy as jnp
        import numpy as np
        B, S, H, HID = (1, 512, 128, 128)
        LN_EPS = 1e-05

        def _layernorm(y, gamma, beta):
            mu = jnp.mean(y, axis=-1, keepdims=True)
            var = jnp.mean(jnp.square(y - mu), axis=-1, keepdims=True)
            return (y - mu) * jax.lax.rsqrt(var + LN_EPS) * gamma + beta
        hi = jnp.einsum('bsh,hk->bsk', x, W1[:H])
        hj = jnp.einsum('bsh,hk->bsk', x, W1[H:])
        h = jax.nn.relu(hi[:, :, None, :] + hj[:, None, :, :] + b1)
        y = jnp.einsum('bijk,kl->bijl', h, W2) + b2
        y = _layernorm(y, gamma, beta)
        out = jnp.einsum('bij,bijh->bih', adj, y)
        return out

    def _L2_gnn_ref(x, adj, theta, bias):
        import jax, jax.numpy as jnp
        import numpy as np
        BS, N, D_IN, D_OUT = (8, 1024, 128, 128)
        n = adj.shape[1]
        adj = adj + jnp.eye(n, dtype=adj.dtype)
        deg = jnp.sum(adj, axis=2)
        d_inv_sqrt = 1.0 / jnp.sqrt(deg)
        adj_norm = adj * d_inv_sqrt[:, :, None] * d_inv_sqrt[:, None, :]
        support = jnp.einsum('bni,io->bno', x, theta)
        out = jnp.einsum('bnm,bmo->bno', adj_norm, support) + bias
        return out

    def _L3_gnn_ref(x, adjacency, node_mask, W1, b1, W2, b2, eps):
        import jax, jax.numpy as jnp
        import numpy as np
        B, N, F, H = (16, 512, 128, 128)
        x_agg = jnp.einsum('bnf,bnm->bmf', x, adjacency)
        h = (1.0 + eps) * x + x_agg
        y = jnp.maximum(h @ W1 + b1, 0.0) @ W2 + b2
        return jnp.where(node_mask[..., None], y, jnp.zeros((), dtype=y.dtype))
    h = jnp.maximum(_layernorm(x, axis=-1), 0.0)
    x = x + _L0_gnn_ref(h, adj, L0_gnn_W, L0_gnn_b)
    h = jnp.maximum(_layernorm(x, axis=-1), 0.0)
    x = x + _L1_gnn_ref(h, adj, L1_gnn_W1, L1_gnn_b1, L1_gnn_W2, L1_gnn_b2, L1_gnn_gamma, L1_gnn_beta)
    h = jnp.maximum(_layernorm(x, axis=-1), 0.0)
    x = x + _L2_gnn_ref(h, adj, L2_gnn_theta, L2_gnn_bias)
    h = jnp.maximum(_layernorm(x, axis=-1), 0.0)
    x = x + _L3_gnn_ref(h, adj, nodemask, L3_gnn_W1, L3_gnn_b1, L3_gnn_W2, L3_gnn_b2, L3_gnn_eps)
    return x

_drawn_inputs = setup_inputs


def setup_inputs(seed=0):
    import zlib

    import numpy as np

    out = dict(_drawn_inputs(seed))
    spreads = {'L1_gnn_b1': (0.0, 0.1),
     'L1_gnn_b2': (0.0, 0.1),
     'L1_gnn_gamma': (1.0, 0.2),
     'L1_gnn_beta': (0.0, 0.1),
     'L3_gnn_b1': (0.0, 2.0),
     'L3_gnn_b2': (0.0, 0.8)}
    factors = {'L0_gnn_b': 4.085, 'L2_gnn_bias': 8.0}
    for name, (base, spread) in spreads.items():
        noise = np.random.default_rng([zlib.crc32(name.encode()), seed]).standard_normal(out[name].shape)
        drawn = base * np.exp(spread * noise) if base else spread * noise
        out[name] = jnp.asarray(drawn.astype(out[name].dtype))
    for name, factor in factors.items():
        out[name] = (out[name] * factor).astype(out[name].dtype)
    return out
```

```python
from contextlib import ExitStack

import concourse.bass as bass
from concourse import mybir

F32 = mybir.dt.float32
BF16 = mybir.dt.bfloat16
F16 = mybir.dt.float16
U8 = mybir.dt.uint8
ALU = mybir.AluOpType
ACT = mybir.ActivationFunctionType
AX = mybir.AxisListType

P = 128
GRAPHS = 64
EPS = 1e-5
NB = 4
CW = NB * P
SLOTS = 4
ROUNDS = GRAPHS // (NB * SLOTS)
CHUNKS = GRAPHS // NB

UG = 8
GW = UG * P
GROUPS = GRAPHS * P // UG
RING = 4
ITERS = GROUPS // RING
GPG = P // UG
QUAD = 4
QUADS = P // QUAD
PARTS = 3
DVE_UNITS = 1
ACT_UNITS = UG - DVE_UNITS
AHEAD = 3
SZ = 64.0
SW = 64.0


def gnn_stack(nc, x, adj, nodemask, w0, b0, w1, b1, w2, b2, gamma, beta, theta, bias2,
              w31, b31, w32, b32, eps3, out):
    a_scratch = nc.dram_tensor("a_scratch", [GRAPHS, PARTS, P, P], BF16, kind="Internal").ap()

    with ExitStack() as ctx:
        def sb(name, shape, dt=F32):
            return ctx.enter_context(nc.sbuf_tensor(name, shape, dt))

        def sem(name):
            return ctx.enter_context(nc.semaphore(name))

        X = sb("X", [P, GRAPHS * P])
        ADJT = sb("ADJT", [P, GRAPHS * P])
        NAT = sb("NAT", [P, GRAPHS * P])
        BT = sb("BT", [P, GRAPHS * P])
        S = sb("S", [P, GRAPHS])
        DINV = sb("DINV", [P, GRAPHS])
        DSQ = sb("DSQ", [P, GRAPHS])
        MASK = sb("MASK", [P, GRAPHS])

        W0 = sb("W0", [P, P]); W1A = sb("W1A", [P, P]); W1B = sb("W1B", [P, P]); W2 = sb("W2", [P, P])
        W2C = sb("W2C", [P, P])
        NW2C = sb("NW2C", [P, P])
        TH = sb("TH", [P, P]); W31 = sb("W31", [P, P]); W32 = sb("W32", [P, P])
        B0R = sb("B0R", [P, P]); B2R = sb("B2R", [P, P]); BETAR = sb("BETAR", [P, P])
        BIAS2R = sb("BIAS2R", [P, P]); B32R = sb("B32R", [P, P])
        B2C = sb("B2C", [P, P])
        B1 = sb("B1", [P, 1]); NB1 = sb("NB1", [P, 1]); B31 = sb("B31", [P, 1])
        GAM = sb("GAM", [P, 1]); E3 = sb("E3", [P, 1]); E3P1 = sb("E3P1", [P, 1]); EPSC = sb("EPSC", [P, 1])
        MEANS = sb("MEANS", [P, 4])
        IDENT = sb("IDENT", [P, P])
        GAMS = sb("GAMS", [P, 1])
        DIAGE = sb("DIAGE", [P, P])
        NHALF = sb("NHALF", [P, UG])
        MRAW = sb("MRAW", [GRAPHS, P], U8); MROW = sb("MROW", [GRAPHS, P])
        SEL = sb("SEL", [P, QUADS, P], BF16)

        RINGS = 4 * SLOTS * CW
        ARENA = sb("ARENA", [P, RINGS + SLOTS * CW + SLOTS * CW * PARTS // 2])

        def share(first, words, dt=F32):
            t = ARENA[:, first:first + words]
            return t if dt == F32 else t.bitcast(dt)

        H, TT, T1, AF = ([share((k * SLOTS + c) * CW, CW).rearrange("p (b l) -> p b l", b=NB) for c in range(SLOTS)]
                         for k in range(4))
        ADJ = [share(RINGS + c * CW, CW).rearrange("p (b l) -> p b l", b=NB) for c in range(SLOTS)]
        APART = [share(RINGS + SLOTS * CW + c * CW * PARTS // 2, CW * PARTS // 2, BF16)
                 .rearrange("p (b t l) -> p b t l", b=NB, t=PARTS) for c in range(SLOTS)]

        def slots(name, shape):
            return [sb(f"{name}{c}", shape) for c in range(SLOTS)]
        ST = slots("ST", [P, NB, 6]); MV = slots("MV", [P, NB, 2])
        SD = slots("SD", [P, NB]); RS = slots("RS", [P, NB]); NM = slots("NM", [P, NB])
        RSD = slots("RSD", [P, NB]); NMD = slots("NMD", [P, NB])

        HID = share(0, RING * GW).rearrange("p (r u j) -> p r u j", r=RING, u=UG)
        ZH = share(RING * GW, RING * GW // 2, F16).rearrange("p (r u l) -> p r u l", r=RING, u=UG)
        ZL = share(RING * GW * 3 // 2, RING * GW // 2, F16).rearrange("p (r u l) -> p r u l", r=RING, u=UG)
        JUNK = share(RINGS + SLOTS * CW, ACT_UNITS * P, BF16).rearrange("p (r u l) -> p r u l", r=2, u=ACT_UNITS)
        AROWS = sb("AROWS", [P, 2, QUAD * P], BF16)
        STZ = sb("STZ", [P, RING, DVE_UNITS, 6])
        VAR = sb("VAR", [P, RING, UG, 2])
        VE = sb("VE", [P, RING, UG]); RSTD = sb("RSTD", [P, RING, UG]); W32F = sb("W32F", [P, RING, UG])
        W16 = sb("W16", [P, RING, UG, 2], F16)

        PS = ctx.enter_context(nc.psum_tensor("PS", [P, 8, 512], F32))

        def bank(c, k):
            return PS[:, 2 * c + k, :].rearrange("p (b l) -> p b l", b=NB)

        def chunk(t, n):
            return t[:, bass.ds(n * CW, CW)].rearrange("p (b l) -> p b l", b=NB)

        def graph_at(base):
            if isinstance(base, int):
                return base * RING // GPG
            return nc.s_assert_within(base >> 2, 0, GRAPHS - 1,
                                      skip_runtime_bounds_check_because="base is below ITERS")

        def rows4(t):
            return t[:, :].rearrange("p (o l) -> p o l", o=1).broadcast_to([P, NB, P])

        def cols4(t, n):
            return t[:, bass.ds(n * NB, NB)].rearrange("p (b o) -> p b o", o=1).broadcast_to([P, NB, P])

        weights_in = sem("weights_in"); passed = sem("passed")
        const_step = sem("const_step"); pool_const = sem("pool_const"); ident_ready = sem("ident_ready")
        setup_step = sem("setup_step"); setup_done = sem("setup_done")
        mask_turned = sem("mask_turned")
        loaded = [sem(f"loaded{c}") for c in range(SLOTS)]
        reloaded = [sem(f"reloaded{c}") for c in range(SLOTS)]
        a_stored = [sem(f"a_stored{c}") for c in range(SLOTS)]
        out_stored = [sem(f"out_stored{c}") for c in range(SLOTS)]

        class Norm:
            def __init__(self, n):
                self.stats, self.var, self.std, self.rstd, self.scale, self.scaled, self.h = (
                    sem(f"ln{n}_{s}") for s in ("stats", "var", "std", "rstd", "scale", "scaled", "h"))
        ln = [Norm(n) for n in range(4)]

        adj_turned = sem("adj_turned"); adjt_kept = sem("adjt_kept"); rowsum = sem("rowsum")
        l0_agg = sem("l0_agg"); l0_agg_copied = sem("l0_agg_copied"); l0_out = sem("l0_out")
        l0_biased = sem("l0_biased"); x1_ready = sem("x1_ready")
        h_turned = sem("h_turned"); h_turned_copied = sem("h_turned_copied")
        ab_ready = sem("ab_ready"); na_kept = sem("na_kept"); b_kept = sem("b_kept")
        a_prod = sem("a_prod"); a_full = sem("a_full"); a_part0 = sem("a_part0")
        a_rest = sem("a_rest"); a_part1 = sem("a_part1"); a_part2 = sem("a_part2")

        rows_in = sem("rows_in"); hid_ready = sem("hid_ready"); z_ready = sem("z_ready")
        zl_ready = sem("zl_ready")
        act_used = sem("act_used")
        bn_done = sem("bn_done"); var_ready = sem("var_ready")
        weight_step = sem("weight_step"); weight_ready = sem("weight_ready")
        ring_free = sem("ring_free"); u_free = sem("u_free")

        deg_ready = sem("deg_ready"); deg_root = sem("deg_root"); dinv_ready = sem("dinv_ready")
        beta_prod = sem("beta_prod"); beta_added = sem("beta_added"); u_scaled = sem("u_scaled"); u_turned = sem("u_turned")
        x2_ready = sem("x2_ready"); bias_added = sem("bias_added")
        l2_agg = sem("l2_agg"); l2_agg_copied = sem("l2_agg_copied"); l2_out = sem("l2_out")
        l2_normed = sem("l2_normed"); x3_ready = sem("x3_ready")
        l3_agg = sem("l3_agg"); l3_agg_copied = sem("l3_agg_copied"); l3_mid = sem("l3_mid")
        l3_relu = sem("l3_relu"); l3_out = sem("l3_out"); l3_biased = sem("l3_biased")
        l3_masked = sem("l3_masked"); x4_ready = sem("x4_ready")

        WEIGHT_LOADS = 17

        def wait_apart(eng, semaphore, count):
            eng.wait_ge(semaphore, count)
            eng.sem_inc(passed, 1)

        block = ctx.enter_context(nc.Block())

        @block.sync
        def _(sp):
            def column(v):
                return v.rearrange("(p o) -> p o", o=1)

            def everywhere(v):
                return v.rearrange("(o l) -> o l", o=1).broadcast_to([P, P])

            def load(n, c):
                sp.dma_start(chunk(X, n), x[bass.ds(n * NB, NB)].rearrange("b n f -> n b f")).then_inc(loaded[c], 16)
                sp.dma_start(ADJ[c][:], adj[bass.ds(n * NB, NB)].rearrange("b n f -> n b f")).then_inc(loaded[c], 16)

            def store_a(n, c):
                sp.wait_ge(a_part2, n + 1)
                sp.dma_start(a_scratch[bass.ds(n * NB, NB)].rearrange("b t i l -> i (b t) l"),
                             APART[c][:].rearrange("p b t l -> p (b t) l")).then_inc(a_stored[c], 16)

            for c in range(SLOTS):
                load(c, c)
                sp.sem_inc(a_stored[c], 16)
            for dst, src in ((W0, w0), (W1A, w1[0:P]), (W1B, w1[P:2 * P]), (W2, w2), (TH, theta),
                             (W31, w31), (W32, w32), (B0R, everywhere(b0)), (B2R, everywhere(b2)),
                             (BETAR, everywhere(beta)), (BIAS2R, everywhere(bias2)), (B32R, everywhere(b32)),
                             (B1, column(b1)), (B31, column(b31)), (GAM, column(gamma)),
                             (E3, eps3.rearrange("(o l) -> o l", o=1).broadcast_to([P, 1])), (MRAW, nodemask)):
                sp.dma_start(dst[:], src).then_inc(weights_in, 16)
            with sp.Fori(1, ROUNDS) as r:
                for c in range(SLOTS):
                    sp.wait_ge(adj_turned, r * SLOTS + (c + 1 - SLOTS))
                    sp.wait_ge(rowsum, r * SLOTS + (c + 1 - SLOTS))
                    load(r * SLOTS + c, c)
                for c in range(SLOTS):
                    store_a((r - 1) * SLOTS + c, c)
            for c in range(SLOTS):
                store_a((ROUNDS - 1) * SLOTS + c, c)
            for c in range(SLOTS):
                sp.wait_ge(a_stored[c], 16 * (ROUNDS + 1))

            def load_rows(b, slot):
                sp.dma_start(AROWS[0:PARTS * QUADS, slot, :],
                             a_scratch[b].rearrange("t (q s) l -> (t q) (s l)", s=QUAD)).then_inc(rows_in, 16)

            load_rows(0, 0)
            sp.wait_ge(rows_in, 16)
            load_rows(1, 1)
            with sp.Fori(1, GRAPHS // 2) as t:
                for k in range(2):
                    sp.wait_ge(rows_in, t * 32 + 16 * k)
                    sp.wait_ge(z_ready, t * (4 * GPG) + 2 * GPG * (k - 1))
                    load_rows(t * 2 + k, k)

            def reload(n, c):
                sp.dma_start(ADJ[c][:], adj[bass.ds(n * NB, NB)].rearrange("b n f -> n b f")).then_inc(reloaded[c], 16)

            def store_out(n, c):
                sp.wait_ge(x4_ready, n + 1)
                sp.dma_start(out[bass.ds(n * NB, NB)].rearrange("b n f -> n b f"), chunk(X, n)).then_inc(out_stored[c], 16)

            for c in range(SLOTS):
                reload(c, c)
            with sp.Fori(1, ROUNDS) as r:
                for c in range(SLOTS):
                    sp.wait_ge(l3_agg, r * SLOTS + (c + 1 - SLOTS))
                    reload(r * SLOTS + c, c)
                for c in range(SLOTS):
                    store_out((r - 1) * SLOTS + c, c)
            for c in range(SLOTS):
                store_out((ROUNDS - 1) * SLOTS + c, c)
            for c in range(SLOTS):
                sp.wait_ge(out_stored[c], 16 * ROUNDS)

        @block.gpsimd
        def _(pool):
            nc.gpsimd.memset(IDENT[:], 0.0).then_inc(const_step, 1)
            nc.gpsimd.memset(SEL[:], 0.0).then_inc(const_step, 1)
            nc.gpsimd.memset(AROWS[:], 0.0).then_inc(pool_const, 1)
            nc.gpsimd.memset(NHALF[:], -0.5).then_inc(pool_const, 1)
            nc.gpsimd.memset(EPSC[:], EPS).then_inc(pool_const, 1)
            pool.wait_ge(const_step, 2)
            nc.gpsimd.affine_select(out=IDENT[:], in_=IDENT[:], compare_op=ALU.not_equal, fill=1.0, base=0,
                                    pattern=[[-1, P]], channel_multiplier=1).then_inc(ident_ready, 1)
            for t in range(PARTS):
                pool.wait_ge(const_step, 2 + t)
                nc.gpsimd.affine_select(out=SEL[:], in_=SEL[:], compare_op=ALU.not_equal, fill=1.0, base=-QUADS * t,
                                        pattern=[[-1, QUADS], [0, P]], channel_multiplier=1).then_inc(const_step, 1)

            with pool.Fori(0, ROUNDS) as r:
                for c in range(SLOTS):
                    n = r * SLOTS + c
                    pool.wait_ge(a_part0, n + 1)
                    nc.gpsimd.tensor_tensor(AF[c][:], AF[c][:], APART[c][:, :, 0, :], ALU.subtract).then_inc(a_rest, 1)
                for c in range(SLOTS):
                    n = r * SLOTS + c
                    pool.wait_ge(a_part1, n + 1)
                    nc.gpsimd.tensor_tensor(APART[c][:, :, 2, :], AF[c][:], APART[c][:, :, 1, :],
                                            ALU.subtract).then_inc(a_part2, 1)

            pool.wait_ge(adjt_kept, CHUNKS)
            pool.wait_ge(pool_const, 3)
            with pool.Fori(0, ITERS) as it:
                for s in range(RING):
                    g1 = it * RING + (s + 1)
                    pool.wait_ge(act_used, it * (2 * RING) + 2 * (s + 1))
                    wait_apart(pool, var_ready, g1)
                    nc.gpsimd.tensor_scalar(VE[:, s], VAR[:, s, :, 1], 1.0 / (SZ * SZ * SW * SW), EPS / (SW * SW),
                                            ALU.mult, ALU.add).then_inc(weight_step, 1)
                    pool.wait_ge(weight_step, it * (3 * RING) + (3 * s + 1))
                    nc.gpsimd.tensor_tensor(RSTD[:, s], VE[:, s], NHALF[:], ALU.pow).then_inc(weight_step, 1)
                    pool.wait_ge(weight_step, it * (3 * RING) + (3 * s + 2))
                    turned = ADJT[:, bass.ds(it * (RING * UG) + s * UG, UG)]
                    nc.gpsimd.tensor_tensor(W32F[:, s], RSTD[:, s], turned, ALU.mult)
                    nc.gpsimd.tensor_tensor(W16[:, s, :, 0], RSTD[:, s], turned, ALU.mult).then_inc(weight_step, 1)
                    pool.wait_ge(weight_step, it * (3 * RING) + (3 * s + 3))
                    nc.gpsimd.tensor_tensor(W16[:, s, :, 1], W32F[:, s], W16[:, s, :, 0],
                                            ALU.subtract).then_inc(weight_ready, 1)

            pool.wait_ge(u_free, GROUPS // 2 + 2)
            with pool.Fori(0, ROUNDS) as r:
                for c in range(SLOTS):
                    n = r * SLOTS + c
                    if c == 0:
                        pool.wait_ge(rowsum, CHUNKS)
                    nc.gpsimd.tensor_tensor(T1[c][:], rows4(BETAR), cols4(S, n), ALU.mult).then_inc(beta_prod, 1)
                for c in range(SLOTS):
                    n = r * SLOTS + c
                    pool.wait_ge(beta_prod, n + 1)
                    nc.gpsimd.tensor_tensor(chunk(X, n), chunk(X, n), T1[c][:], ALU.add).then_inc(beta_added, 1)
                for c in range(SLOTS):
                    n = r * SLOTS + c
                    wait_apart(pool, ln[2].h, n + 1)
                    nc.gpsimd.tensor_tensor(chunk(X, n), chunk(X, n), rows4(BIAS2R), ALU.add).then_inc(bias_added, 1)
                pool.wait_ge(x4_ready, r * SLOTS + SLOTS)

        @block.scalar
        def _(act):
            def norm_std(L, c, n):
                act.wait_ge(L.var, n + 1)
                nc.scalar.activation(SD[c][:], MV[c][:, :, 1], ACT.Sqrt, bias=EPSC[:, 0:1]).then_inc(L.std, 1)

            def norm_relu(L, c, n, rs, nm, ready):
                wait_apart(act, ready, n + 1)
                for b in range(NB):
                    ins = nc.scalar.activation(H[c][:, b, :], X[:, bass.ds(n * CW + b * P, P)], ACT.Relu,
                                               bias=nm[c][:, b:b + 1], scale=rs[c][:, b:b + 1])
                ins.then_inc(L.h, 1)

            act.wait_ge(pool_const, 3)
            act.wait_ge(setup_done, 1)
            with act.Fori(0, ROUNDS) as r:
                for c in range(SLOTS):
                    n = r * SLOTS + c
                    act.wait_ge(adj_turned, n + 1)
                    nc.scalar.activation(chunk(ADJT, n), bank(c, 0), ACT.Copy).then_inc(adjt_kept, 1)
                for c in range(SLOTS):
                    norm_std(ln[0], c, r * SLOTS + c)
                for c in range(SLOTS):
                    norm_relu(ln[0], c, r * SLOTS + c, RS, NM, ln[0].scale)
                for c in range(SLOTS):
                    n = r * SLOTS + c
                    act.wait_ge(l0_agg, n + 1)
                    nc.scalar.activation(TT[c][:], bank(c, 1), ACT.Copy).then_inc(l0_agg_copied, 1)
                for c in range(SLOTS):
                    norm_std(ln[1], c, r * SLOTS + c)
                for c in range(SLOTS):
                    norm_relu(ln[1], c, r * SLOTS + c, RS, NM, ln[1].scale)
                for c in range(SLOTS):
                    n = r * SLOTS + c
                    act.wait_ge(h_turned, n + 1)
                    nc.scalar.activation(TT[c][:], bank(c, 1), ACT.Copy).then_inc(h_turned_copied, 1)
                for c in range(SLOTS):
                    n = r * SLOTS + c
                    act.wait_ge(ab_ready, n + 1)
                    act.wait_ge(a_stored[c], r * 16 + 16)
                    nc.scalar.activation(H[c][:], bank(c, 0), ACT.Identity, bias=NB1[:, 0:1], scale=-1.0)
                    nc.scalar.activation(chunk(NAT, n), bank(c, 0), ACT.Identity, bias=NB1[:, 0:1],
                                         scale=-1.0).then_inc(na_kept, 1)
                for c in range(SLOTS):
                    n = r * SLOTS + c
                    act.wait_ge(a_full, n + 1)
                    nc.scalar.activation(APART[c][:, :, 0, :], AF[c][:], ACT.Copy).then_inc(a_part0, 1)
                for c in range(SLOTS):
                    n = r * SLOTS + c
                    act.wait_ge(a_rest, n + 1)
                    nc.scalar.activation(APART[c][:, :, 1, :], AF[c][:], ACT.Copy).then_inc(a_part1, 1)

            for c in range(SLOTS):
                act.wait_ge(a_stored[c], 16 * (ROUNDS + 1))
            with act.Fori(0, ITERS) as it:
                for s in range(RING):
                    zb = 2 * (s % 2)
                    act.wait_ge(z_ready, it * (2 * RING) + 2 * (s + 1))
                    act.wait_ge(ring_free, it * RING + (s + 1))
                    nc.scalar.activation(ZH[:, s].rearrange("p u l -> p (u l)"),
                                         PS[:, zb:zb + 2, :].rearrange("p a l -> p (a l)"), ACT.Copy)
                    for u in range(ACT_UNITS):
                        ins = nc.scalar.activation(JUNK[:, s % 2, u, :], PS[:, zb + u // QUAD, (u % QUAD) * P:(u % QUAD + 1) * P],
                                                   ACT.Square, scale=float(P) ** -0.5,
                                                   accum_out=VAR[:, s, u, 1:2])
                        if u in (QUAD - 1, ACT_UNITS - 1):
                            ins.then_inc(act_used, 1)

            act.wait_ge(deg_ready, 1)
            nc.scalar.activation(DSQ[:], DINV[:], ACT.Sqrt).then_inc(deg_root, 1)
            act.wait_ge(u_free, GROUPS // 2 + 2)
            with act.Fori(0, ROUNDS) as r:
                for c in range(SLOTS):
                    n = r * SLOTS + c
                    nc.scalar.activation(AF[c][:], chunk(NAT, n), ACT.Copy, scale=GAMS[:, 0:1]).then_inc(u_scaled, 1)
                for c in range(SLOTS):
                    norm_std(ln[2], c, r * SLOTS + c)
                for c in range(SLOTS):
                    norm_relu(ln[2], c, r * SLOTS + c, RSD, NMD, ln[2].scaled)
                for c in range(SLOTS):
                    n = r * SLOTS + c
                    act.wait_ge(l2_agg, n + 1)
                    nc.scalar.activation(TT[c][:], bank(c, 1), ACT.Copy).then_inc(l2_agg_copied, 1)
                for c in range(SLOTS):
                    norm_std(ln[3], c, r * SLOTS + c)
                for c in range(SLOTS):
                    norm_relu(ln[3], c, r * SLOTS + c, RS, NM, ln[3].scale)
                for c in range(SLOTS):
                    n = r * SLOTS + c
                    act.wait_ge(l3_agg, n + 1)
                    nc.scalar.activation(TT[c][:], bank(c, 1), ACT.Copy).then_inc(l3_agg_copied, 1)
                for c in range(SLOTS):
                    n = r * SLOTS + c
                    act.wait_ge(l3_mid, n + 1)
                    nc.scalar.activation(AF[c][:], bank(c, 0), ACT.Relu, bias=B31[:, 0:1]).then_inc(l3_relu, 1)
                act.wait_ge(l3_out, r * SLOTS + SLOTS)

        @block.vector
        def _(dve):
            def norm_stats(L, c, n):
                for b in range(NB):
                    ins = nc.vector.bn_stats(ST[c][:, b, :], X[:, bass.ds(n * CW + b * P, P)])
                ins.then_inc(L.stats, 1)

            def norm_var(L, c, n):
                wait_apart(dve, L.stats, n + 1)
                for b in range(NB):
                    ins = nc.vector.bn_aggr(MV[c][:, b, :], ST[c][:, b, :])
                ins.then_inc(L.var, 1)

            def norm_rstd(L, c, n):
                dve.wait_ge(L.std, n + 1)
                nc.vector.reciprocal(RS[c][:], SD[c][:]).then_inc(L.rstd, 1)

            def norm_shift(L, c, n):
                dve.wait_ge(L.rstd, n + 1)
                nc.vector.scalar_tensor_tensor(out=NM[c][:], in0=MV[c][:, :, 0], scalar=-1.0, in1=RS[c][:],
                                               op0=ALU.mult, op1=ALU.mult).then_inc(L.scale, 1)

            dve.wait_ge(weights_in, 16 * WEIGHT_LOADS)
            nc.vector.tensor_reduce(MEANS[:, 0:1], W2[:], AX.X, ALU.add)
            nc.vector.tensor_reduce(MEANS[:, 1:2], B2R[:], AX.X, ALU.add)
            nc.vector.tensor_scalar(NB1[:], B1[:], -1.0, None, ALU.mult)
            nc.vector.tensor_copy(MROW[:], MRAW[:])
            nc.vector.tensor_scalar(E3P1[:], E3[:], 1.0, None, ALU.add).then_inc(setup_step, 1)
            dve.wait_ge(setup_step, 1)
            nc.vector.tensor_scalar(MEANS[:, 2:4], MEANS[:, 0:2], 1.0 / P, None, ALU.mult).then_inc(setup_step, 1)
            dve.wait_ge(setup_step, 2)
            dve.wait_ge(ident_ready, 1)
            nc.vector.tensor_scalar(W2C[:], W2[:], MEANS[:, 2:3], SZ, ALU.subtract, ALU.mult)
            nc.vector.tensor_scalar(NW2C[:], W2[:], MEANS[:, 2:3], -SZ, ALU.subtract, ALU.mult)
            nc.vector.tensor_scalar(B2C[:], B2R[:], MEANS[:, 3:4], SZ, ALU.subtract, ALU.mult)
            nc.vector.tensor_scalar(GAMS[:], GAM[:], 1.0 / (SZ * SW), None, ALU.mult)
            nc.vector.tensor_scalar(DIAGE[:], IDENT[:], E3P1[:, 0:1], None, ALU.mult).then_inc(setup_done, 1)

            with dve.Fori(0, ROUNDS) as r:
                for c in range(SLOTS):
                    dve.wait_ge(loaded[c], r * 32 + 32)
                    norm_stats(ln[0], c, r * SLOTS + c)
                for c in range(SLOTS):
                    norm_var(ln[0], c, r * SLOTS + c)
                for c in range(SLOTS):
                    n = r * SLOTS + c
                    nc.vector.tensor_reduce(S[:, bass.ds(n * NB, NB)], ADJ[c][:], AX.X, ALU.add).then_inc(rowsum, 1)
                for c in range(SLOTS):
                    norm_rstd(ln[0], c, r * SLOTS + c)
                for c in range(SLOTS):
                    norm_shift(ln[0], c, r * SLOTS + c)
                for c in range(SLOTS):
                    n = r * SLOTS + c
                    dve.wait_ge(l0_out, n + 1)
                    nc.vector.tensor_tensor(T1[c][:], bank(c, 0), rows4(B0R), ALU.add).then_inc(l0_biased, 1)
                for c in range(SLOTS):
                    n = r * SLOTS + c
                    dve.wait_ge(l0_biased, n + 1)
                    nc.vector.scalar_tensor_tensor(out=chunk(X, n), in0=T1[c][:], scalar=0.0, in1=chunk(X, n),
                                                   op0=ALU.max, op1=ALU.add).then_inc(x1_ready, 1)
                for c in range(SLOTS):
                    wait_apart(dve, x1_ready, r * SLOTS + (c + 1))
                    norm_stats(ln[1], c, r * SLOTS + c)
                for c in range(SLOTS):
                    norm_var(ln[1], c, r * SLOTS + c)
                for c in range(SLOTS):
                    norm_rstd(ln[1], c, r * SLOTS + c)
                for c in range(SLOTS):
                    norm_shift(ln[1], c, r * SLOTS + c)
                for c in range(SLOTS):
                    n = r * SLOTS + c
                    dve.wait_ge(ab_ready, n + 1)
                    nc.vector.tensor_copy(chunk(BT, n), bank(c, 1)).then_inc(b_kept, 1)
                for c in range(SLOTS):
                    n = r * SLOTS + c
                    dve.wait_ge(a_prod, n + 1)
                    nc.vector.tensor_tensor(AF[c][:], bank(c, 0), rows4(B2C), ALU.add).then_inc(a_full, 1)

            def hidden(base, k, q):
                a = NAT[:, bass.ds(base * (RING * UG) + (k * UG + q * QUAD), QUAD)]
                b = BT[:, bass.ds(graph_at(base) * P, P)]
                nc.vector.tensor_tensor(HID[:, k, q * QUAD:(q + 1) * QUAD],
                                        a.rearrange("p (u o) -> p u o", o=1).broadcast_to([P, QUAD, P]),
                                        b.rearrange("p (o j) -> p o j", o=1).broadcast_to([P, QUAD, P]),
                                        ALU.max).then_inc(hid_ready, 1)

            def keep_u(it, pair):
                dve.wait_ge(ring_free, it * RING + (2 * pair + 2 + RING))
                nc.vector.tensor_reduce(NAT[:, bass.ds(it * (RING * UG) + pair * 2 * UG, 2 * UG)],
                                        PS[:, 6 + pair, 0:4 * UG].rearrange("p (i t) -> p i t", t=2),
                                        AX.X, ALU.add).then_inc(u_free, 1)

            def group(it, s, ahead, keep):
                def low_part(q):
                    dve.wait_ge(act_used, it * (2 * RING) + (2 * s + 1 + q))
                    units = slice(QUAD * q, QUAD * (q + 1))
                    nc.vector.tensor_tensor(ZL[:, s, units].rearrange("p u l -> p (u l)"), PS[:, zb + q, :],
                                            ZH[:, s, units].rearrange("p u l -> p (u l)"),
                                            ALU.subtract).then_inc(zl_ready, 1)

                zb = 2 * (s % 2)
                low_part(0)
                if ahead:
                    hidden(it + (s + AHEAD) // RING, (s + AHEAD) % RING, 0)
                low_part(1)
                for u in range(DVE_UNITS):
                    col = (ACT_UNITS + u) % QUAD * P
                    ins = nc.vector.bn_stats(STZ[:, s, u, :], PS[:, zb + 1, col:col + P])
                ins.then_inc(bn_done, 1)
                if ahead:
                    hidden(it + (s + AHEAD) // RING, (s + AHEAD) % RING, 1)
                if keep and s % 2 == 0:
                    keep_u(it - 1, s // 2)
                wait_apart(dve, bn_done, it * RING + (s + 1))
                for u in range(DVE_UNITS):
                    ins = nc.vector.bn_aggr(VAR[:, s, ACT_UNITS + u, :], STZ[:, s, u, :])
                ins.then_inc(var_ready, 1)

            dve.sem_inc(u_free, 2)
            dve.wait_ge(na_kept, CHUNKS)
            dve.wait_ge(b_kept, CHUNKS)
            dve.wait_ge(a_prod, CHUNKS)
            dve.wait_ge(a_part2, CHUNKS)
            for k in range(AHEAD):
                for q in range(2):
                    hidden(0, k, q)
            for s in range(RING):
                group(0, s, True, False)
            with dve.Fori(1, ITERS - 1) as it:
                for s in range(RING):
                    group(it, s, True, True)
            for s in range(RING):
                group(ITERS - 1, s, s + AHEAD < RING, True)
            for pair in range(2):
                keep_u(ITERS - 1, pair)

            dve.wait_ge(rowsum, CHUNKS)
            nc.vector.tensor_scalar(DINV[:], S[:], 1.0, None, ALU.add).then_inc(deg_ready, 1)
            dve.wait_ge(deg_root, 1)
            nc.vector.reciprocal(DINV[:], DSQ[:]).then_inc(dinv_ready, 1)
            dve.wait_ge(mask_turned, 1)
            nc.vector.tensor_copy(MASK[:], PS[:, 7, 0:GRAPHS]).then_inc(setup_step, 1)
            with dve.Fori(0, ROUNDS) as r:
                for c in range(SLOTS):
                    n = r * SLOTS + c
                    dve.wait_ge(u_turned, n + 1)
                    dve.wait_ge(beta_added, n + 1)
                    nc.vector.tensor_tensor(chunk(X, n), chunk(X, n), bank(c, 0), ALU.add).then_inc(x2_ready, 1)
                for c in range(SLOTS):
                    wait_apart(dve, x2_ready, r * SLOTS + (c + 1))
                    norm_stats(ln[2], c, r * SLOTS + c)
                for c in range(SLOTS):
                    norm_var(ln[2], c, r * SLOTS + c)
                for c in range(SLOTS):
                    norm_rstd(ln[2], c, r * SLOTS + c)
                for c in range(SLOTS):
                    norm_shift(ln[2], c, r * SLOTS + c)
                for c in range(SLOTS):
                    n = r * SLOTS + c
                    dve.wait_ge(ln[2].scale, n + 1)
                    dve.wait_ge(dinv_ready, 1)
                    nc.vector.tensor_tensor(RSD[c][:], RS[c][:], DINV[:, bass.ds(n * NB, NB)], ALU.mult)
                    nc.vector.tensor_tensor(NMD[c][:], NM[c][:], DINV[:, bass.ds(n * NB, NB)],
                                            ALU.mult).then_inc(ln[2].scaled, 1)
                for c in range(SLOTS):
                    n = r * SLOTS + c
                    dve.wait_ge(l2_out, n + 1)
                    nc.vector.tensor_tensor(T1[c][:], bank(c, 0), cols4(DINV, n), ALU.mult).then_inc(l2_normed, 1)
                for c in range(SLOTS):
                    n = r * SLOTS + c
                    dve.wait_ge(l2_normed, n + 1)
                    dve.wait_ge(bias_added, n + 1)
                    nc.vector.tensor_tensor(chunk(X, n), T1[c][:], chunk(X, n), ALU.add).then_inc(x3_ready, 1)
                for c in range(SLOTS):
                    wait_apart(dve, x3_ready, r * SLOTS + (c + 1))
                    norm_stats(ln[3], c, r * SLOTS + c)
                for c in range(SLOTS):
                    norm_var(ln[3], c, r * SLOTS + c)
                for c in range(SLOTS):
                    norm_rstd(ln[3], c, r * SLOTS + c)
                for c in range(SLOTS):
                    norm_shift(ln[3], c, r * SLOTS + c)
                for c in range(SLOTS):
                    n = r * SLOTS + c
                    dve.wait_ge(l3_out, n + 1)
                    nc.vector.tensor_tensor(T1[c][:], bank(c, 1), rows4(B32R), ALU.add).then_inc(l3_biased, 1)
                for c in range(SLOTS):
                    n = r * SLOTS + c
                    dve.wait_ge(l3_biased, n + 1)
                    dve.wait_ge(setup_step, 3)
                    nc.vector.tensor_tensor(T1[c][:], T1[c][:], cols4(MASK, n), ALU.mult).then_inc(l3_masked, 1)
                for c in range(SLOTS):
                    n = r * SLOTS + c
                    dve.wait_ge(l3_masked, n + 1)
                    nc.vector.tensor_tensor(chunk(X, n), T1[c][:], chunk(X, n), ALU.add).then_inc(x4_ready, 1)

        @block.tensor
        def _(pe):
            def four(dst, c, lhs, rhs, *more):
                pairs = [(lhs, rhs), *more]
                for b in range(NB):
                    for k, (l, m) in enumerate(pairs):
                        ins = nc.tensor.matmul(dst[:, b, :], l(b), m(b), start=(k == 0), stop=(k == len(pairs) - 1))
                return ins

            def graph_of(t, n):
                return lambda b: t[:, bass.ds(n * CW + b * P, P)]

            pe.wait_ge(ident_ready, 1)
            pe.wait_ge(setup_done, 1)
            with pe.Fori(0, ROUNDS) as r:
                for c in range(SLOTS):
                    n = r * SLOTS + c
                    pe.wait_ge(loaded[c], r * 32 + 32)
                    for b in range(NB):
                        ins = nc.tensor.transpose(bank(c, 0)[:, b, :], ADJ[c][:, b, :], IDENT[:])
                    ins.then_inc(adj_turned, 1)
                for c in range(SLOTS):
                    n = r * SLOTS + c
                    pe.wait_ge(adjt_kept, n + 1)
                    pe.wait_ge(ln[0].h, n + 1)
                    four(bank(c, 1), c, lambda b: H[c][:, b, :], graph_of(ADJT, n)).then_inc(l0_agg, 1)
                for c in range(SLOTS):
                    n = r * SLOTS + c
                    pe.wait_ge(l0_agg_copied, n + 1)
                    four(bank(c, 0), c, lambda b: TT[c][:, b, :], lambda b: W0[:]).then_inc(l0_out, 1)
                for c in range(SLOTS):
                    n = r * SLOTS + c
                    pe.wait_ge(ln[1].h, n + 1)
                    for b in range(NB):
                        ins = nc.tensor.transpose(bank(c, 1)[:, b, :], H[c][:, b, :], IDENT[:])
                    ins.then_inc(h_turned, 1)
                for c in range(SLOTS):
                    n = r * SLOTS + c
                    pe.wait_ge(h_turned_copied, n + 1)
                    ht = TT[c][:].rearrange("p b l -> p (b l)")
                    nc.tensor.matmul(PS[:, 2 * c, :], W1A[:], ht, start=True, stop=True)
                    nc.tensor.matmul(PS[:, 2 * c + 1, :], W1B[:], ht, start=True, stop=True).then_inc(ab_ready, 1)
                for c in range(SLOTS):
                    n = r * SLOTS + c
                    pe.wait_ge(na_kept, n + 1)
                    for b in range(NB):
                        ins = nc.tensor.matmul(bank(c, 0)[:, b, :], H[c][:, b, :], NW2C[:], start=True, stop=True)
                    ins.then_inc(a_prod, 1)
                pe.wait_ge(b_kept, r * SLOTS + SLOTS)
                pe.wait_ge(a_full, r * SLOTS + SLOTS)

            def product(base, k, first=False):
                graph = graph_at(base)
                if k == 0:
                    pe.wait_ge(rows_in, graph * 16 + 16)
                for q in range(2):
                    pe.wait_ge(hid_ready, base * (2 * RING) + (2 * k + q + 1))
                    if not first and q == 0:
                        pe.wait_ge(zl_ready, base * (2 * RING) + (2 * k - 3))
                    if not first and q == 1:
                        pe.wait_ge(bn_done, base * RING + (k - 1))
                    zq = PS[:, 2 * (k % 2) + q, :]
                    nc.tensor.matmul(zq, SEL[:, bass.ds((base & 3) * (2 * RING) + (2 * k + q), 1), :].rearrange("p o j -> p (o j)"),
                                     AROWS[:, bass.ds(graph & 1, 1), :].rearrange("p o l -> p (o l)"),
                                     start=True, stop=False, skip_group_check=True)
                    for u in range(QUAD):
                        ins = nc.tensor.matmul(zq[:, u * P:(u + 1) * P], HID[:, k, QUAD * q + u, :], W2C[:],
                                               start=False, stop=(u == QUAD - 1), skip_group_check=True)
                    ins.then_inc(z_ready, 1)

            def weighted_sum(base, k):
                pe.wait_ge(weight_ready, base * RING + (k + 1))
                pe.wait_ge(zl_ready, base * (2 * RING) + (2 * k + 2))
                if k % 2 == 0:
                    pe.wait_ge(u_free, base * 2 + (k // 2 + 1))
                for u in range(UG):
                    col = 2 * ((k % 2) * UG + u)
                    nc.tensor.matmul(PS[:, 6 + k // 2, col:col + 2], ZH[:, k, u, :], W16[:, k, u, :],
                                     start=True, stop=False, skip_group_check=True)
                    ins = nc.tensor.matmul(PS[:, 6 + k // 2, col:col + 1], ZL[:, k, u, :], W16[:, k, u, 0:1],
                                           start=False, stop=True, skip_group_check=True)
                ins.then_inc(ring_free, 1)

            pe.wait_ge(pool_const, 3)
            pe.wait_ge(const_step, 2 + PARTS)
            pe.sem_inc(ring_free, RING)
            product(0, 0, first=True)
            product(0, 1, first=True)
            product(0, 2)
            with pe.Fori(0, ITERS - 1) as it:
                for s in range(RING):
                    product(it + (s + 3) // RING, (s + 3) % RING)
                    weighted_sum(it, s)
            product(ITERS - 1, RING - 1)
            for s in range(RING):
                weighted_sum(ITERS - 1, s)

            pe.wait_ge(bn_done, GROUPS)
            pe.wait_ge(u_free, GROUPS // 2 + 2)
            nc.tensor.transpose(PS[:, 7, 0:GRAPHS], MROW[:], IDENT[0:GRAPHS, 0:GRAPHS]).then_inc(mask_turned, 1)
            pe.wait_ge(setup_step, 3)
            with pe.Fori(0, ROUNDS) as r:
                for c in range(SLOTS):
                    n = r * SLOTS + c
                    pe.wait_ge(u_scaled, n + 1)
                    for b in range(NB):
                        ins = nc.tensor.transpose(bank(c, 0)[:, b, :], AF[c][:, b, :], IDENT[:])
                    ins.then_inc(u_turned, 1)
                for c in range(SLOTS):
                    n = r * SLOTS + c
                    pe.wait_ge(ln[2].h, n + 1)
                    four(bank(c, 1), c, lambda b: H[c][:, b, :], graph_of(ADJT, n),
                         (lambda b: H[c][:, b, :], lambda b: IDENT[:])).then_inc(l2_agg, 1)
                for c in range(SLOTS):
                    n = r * SLOTS + c
                    pe.wait_ge(l2_agg_copied, n + 1)
                    four(bank(c, 0), c, lambda b: TT[c][:, b, :], lambda b: TH[:]).then_inc(l2_out, 1)
                for c in range(SLOTS):
                    n = r * SLOTS + c
                    pe.wait_ge(ln[3].h, n + 1)
                    pe.wait_ge(reloaded[c], r * 16 + 16)
                    four(bank(c, 1), c, lambda b: H[c][:, b, :], lambda b: ADJ[c][:, b, :],
                         (lambda b: H[c][:, b, :], lambda b: DIAGE[:])).then_inc(l3_agg, 1)
                for c in range(SLOTS):
                    n = r * SLOTS + c
                    pe.wait_ge(l3_agg_copied, n + 1)
                    nc.tensor.matmul(PS[:, 2 * c, :], W31[:], TT[c][:].rearrange("p b l -> p (b l)"),
                                     start=True, stop=True).then_inc(l3_mid, 1)
                for c in range(SLOTS):
                    n = r * SLOTS + c
                    pe.wait_ge(l3_relu, n + 1)
                    four(bank(c, 1), c, lambda b: AF[c][:, b, :], lambda b: W32[:]).then_inc(l3_out, 1)
                pe.wait_ge(l3_biased, r * SLOTS + SLOTS)


_ARGS = ["x", "adj", "nodemask", "L0_gnn_W", "L0_gnn_b", "L1_gnn_W1", "L1_gnn_b1", "L1_gnn_W2", "L1_gnn_b2",
         "L1_gnn_gamma", "L1_gnn_beta", "L2_gnn_theta", "L2_gnn_bias", "L3_gnn_W1", "L3_gnn_b1", "L3_gnn_W2",
         "L3_gnn_b2", "L3_gnn_eps"]


def kernel(**inputs):
    import numpy as _np
    import concourse.bacc as _bacc
    from concourse import mybir as _mybir
    from concourse.bass_utils import run_bass_kernel_spmd as _run

    nc = _bacc.Bacc("TRN2", target_bir_lowering=False, num_devices=1)
    arrays, args = {}, []
    for name in _ARGS:
        a = _np.ascontiguousarray(inputs[name])
        if a.dtype == _np.bool_:
            a = a.view(_np.uint8)
        arrays[f"in_{name}"] = a
        args.append(nc.dram_tensor(f"in_{name}", a.shape, _mybir.dt.from_np(a.dtype), kind="ExternalInput").ap())
    out = nc.dram_tensor("out_x", (GRAPHS, P, P), F32, kind="ExternalOutput").ap()
    gnn_stack(nc, *args, out)
    r = _run(nc, [arrays], core_ids=[0])
    return r.results[0]["out_x"]
```

```python
from contextlib import ExitStack

import concourse.bass as bass
from concourse import mybir

F32 = mybir.dt.float32
BF16 = mybir.dt.bfloat16
F16 = mybir.dt.float16
U8 = mybir.dt.uint8
ALU = mybir.AluOpType
ACT = mybir.ActivationFunctionType
AX = mybir.AxisListType

P = 128
GRAPHS = 64
EPS = 1e-5
NB = 4
CW = NB * P
SLOTS = 4
ROUNDS = GRAPHS // (NB * SLOTS)
CHUNKS = GRAPHS // NB

UG = 8
GW = UG * P
GROUPS = GRAPHS * P // UG
RING = 4
ZRING = 3
BODY = RING * ZRING
HEAD = GROUPS % BODY
ITERS = (GROUPS - HEAD) // BODY
assert HEAD == RING
GPG = P // UG
QUAD = 4
QUADS = P // QUAD
PARTS = 3
DVE_UNITS = 1
ACT_UNITS = UG - DVE_UNITS
SZ = 64.0
SW = 64.0


def gnn_stack(nc, x, adj, nodemask, w0, b0, w1, b1, w2, b2, gamma, beta, theta, bias2,
              w31, b31, w32, b32, eps3, out):
    a_scratch = nc.dram_tensor("a_scratch", [GRAPHS, PARTS, P, P], BF16, kind="Internal").ap()

    with ExitStack() as ctx:
        def sb(name, shape, dt=F32):
            return ctx.enter_context(nc.sbuf_tensor(name, shape, dt))

        def sem(name):
            return ctx.enter_context(nc.semaphore(name))

        X = sb("X", [P, GRAPHS * P])
        ADJT = sb("ADJT", [P, GRAPHS * P])
        NAT = sb("NAT", [P, GRAPHS * P])
        BT = sb("BT", [P, GRAPHS * P])
        S = sb("S", [P, GRAPHS])
        DINV = sb("DINV", [P, GRAPHS])
        DSQ = sb("DSQ", [P, GRAPHS])
        MASK = sb("MASK", [P, GRAPHS])

        W0 = sb("W0", [P, P]); W1A = sb("W1A", [P, P]); W1B = sb("W1B", [P, P]); W2 = sb("W2", [P, P])
        W2C = sb("W2C", [P, P])
        NW2C = sb("NW2C", [P, P])
        TH = sb("TH", [P, P]); W31 = sb("W31", [P, P]); W32 = sb("W32", [P, P])
        B0R = sb("B0R", [P, P]); B2R = sb("B2R", [P, P]); BETAR = sb("BETAR", [P, P])
        BIAS2R = sb("BIAS2R", [P, P]); B32R = sb("B32R", [P, P])
        B2C = sb("B2C", [P, P])
        B1 = sb("B1", [P, 1]); NB1 = sb("NB1", [P, 1]); B31 = sb("B31", [P, 1])
        GAM = sb("GAM", [P, 1]); E3 = sb("E3", [P, 1]); E3P1 = sb("E3P1", [P, 1]); EPSC = sb("EPSC", [P, 1])
        MEANS = sb("MEANS", [P, 4])
        IDENT = sb("IDENT", [P, P])
        GAMS = sb("GAMS", [P, 1])
        DIAGE = sb("DIAGE", [P, P])
        NHALF = sb("NHALF", [P, UG])
        MRAW = sb("MRAW", [GRAPHS, P], U8); MROW = sb("MROW", [GRAPHS, P])
        SEL = sb("SEL", [P, QUADS, P], BF16)

        RINGS = 4 * SLOTS * CW
        assert 2 * RING * GW <= RINGS
        ARENA = sb("ARENA", [P, RINGS + SLOTS * CW + SLOTS * CW * PARTS // 2])

        def share(first, words, dt=F32):
            t = ARENA[:, first:first + words]
            return t if dt == F32 else t.bitcast(dt)

        H, TT, T1, AF = ([share((k * SLOTS + c) * CW, CW).rearrange("p (b l) -> p b l", b=NB) for c in range(SLOTS)]
                         for k in range(4))
        ADJ = [share(RINGS + c * CW, CW).rearrange("p (b l) -> p b l", b=NB) for c in range(SLOTS)]
        APART = [share(RINGS + SLOTS * CW + c * CW * PARTS // 2, CW * PARTS // 2, BF16)
                 .rearrange("p (b t l) -> p b t l", b=NB, t=PARTS) for c in range(SLOTS)]

        def slots(name, shape):
            return [sb(f"{name}{c}", shape) for c in range(SLOTS)]
        ST = slots("ST", [P, NB, 6]); MV = slots("MV", [P, NB, 2])
        SD = slots("SD", [P, NB]); RS = slots("RS", [P, NB]); NM = slots("NM", [P, NB])
        RSD = slots("RSD", [P, NB]); NMD = slots("NMD", [P, NB])

        HID = share(0, RING * GW).rearrange("p (r u j) -> p r u j", r=RING, u=UG)
        ZH = share(RING * GW, RING * GW // 2, F16).rearrange("p (r u l) -> p r u l", r=RING, u=UG)
        ZL = share(RING * GW * 3 // 2, RING * GW // 2, F16).rearrange("p (r u l) -> p r u l", r=RING, u=UG)
        JUNK = share(RINGS + SLOTS * CW, RING * ACT_UNITS * P // 2, BF16).rearrange("p (r u l) -> p r u l", r=RING, u=ACT_UNITS)
        AROWS = sb("AROWS", [P, 2, QUAD * P], BF16)
        STZ = sb("STZ", [P, RING, DVE_UNITS, 6])
        VAR = sb("VAR", [P, RING, UG, 2])
        VE = sb("VE", [P, RING, UG]); RSTD = sb("RSTD", [P, RING, UG]); W32F = sb("W32F", [P, RING, UG])
        W16 = sb("W16", [P, RING, UG, 2], F16)

        PS = ctx.enter_context(nc.psum_tensor("PS", [P, 8, 512], F32))

        def bank(c, k):
            return PS[:, 2 * c + k, :].rearrange("p (b l) -> p b l", b=NB)

        def chunk(t, n):
            return t[:, bass.ds(n * CW, CW)].rearrange("p (b l) -> p b l", b=NB)

        def group_at(it, k):
            return it * BODY + (HEAD + k)

        def slot(k):
            return (HEAD + k) % RING

        def zslot(k):
            return (HEAD + k) % ZRING

        def pair_bank(k):
            return 6 + k // 2 % 2

        def graph_of_group(g):
            if isinstance(g, int):
                return g // GPG
            return nc.s_assert_within(g >> (GPG.bit_length() - 1), 0, GRAPHS - 1,
                                      skip_runtime_bounds_check_because="g is below GROUPS")

        def rows4(t):
            return t[:, :].rearrange("p (o l) -> p o l", o=1).broadcast_to([P, NB, P])

        def cols4(t, n):
            return t[:, bass.ds(n * NB, NB)].rearrange("p (b o) -> p b o", o=1).broadcast_to([P, NB, P])

        weights_in = sem("weights_in"); passed = sem("passed")
        const_step = sem("const_step"); pool_const = sem("pool_const"); ident_ready = sem("ident_ready")
        setup_step = sem("setup_step"); setup_done = sem("setup_done")
        mask_turned = sem("mask_turned")
        loaded = [sem(f"loaded{c}") for c in range(SLOTS)]
        reloaded = [sem(f"reloaded{c}") for c in range(SLOTS)]
        a_stored = [sem(f"a_stored{c}") for c in range(SLOTS)]
        out_stored = [sem(f"out_stored{c}") for c in range(SLOTS)]

        class Norm:
            def __init__(self, n):
                self.stats, self.var, self.std, self.rstd, self.scale, self.scaled, self.h = (
                    sem(f"ln{n}_{s}") for s in ("stats", "var", "std", "rstd", "scale", "scaled", "h"))
        ln = [Norm(n) for n in range(4)]

        adj_turned = sem("adj_turned"); adjt_kept = sem("adjt_kept"); rowsum = sem("rowsum")
        l0_agg = sem("l0_agg"); l0_agg_copied = sem("l0_agg_copied"); l0_out = sem("l0_out")
        l0_biased = sem("l0_biased"); x1_ready = sem("x1_ready")
        h_turned = sem("h_turned"); h_turned_copied = sem("h_turned_copied")
        ab_ready = sem("ab_ready"); na_kept = sem("na_kept"); b_kept = sem("b_kept")
        a_prod = sem("a_prod"); a_full = sem("a_full"); a_part0 = sem("a_part0")
        a_rest = sem("a_rest"); a_part1 = sem("a_part1"); a_part2 = sem("a_part2")

        rows_in = sem("rows_in"); hid_ready = sem("hid_ready"); z_ready = sem("z_ready")
        zl_ready = sem("zl_ready")
        act_used = sem("act_used")
        bn_done = sem("bn_done"); var_ready = sem("var_ready")
        weight_step = sem("weight_step"); weight_high = sem("weight_high"); weight_ready = sem("weight_ready")
        ring_free = sem("ring_free"); u_free = sem("u_free")

        deg_ready = sem("deg_ready"); deg_root = sem("deg_root"); dinv_ready = sem("dinv_ready")
        beta_prod = sem("beta_prod"); beta_added = sem("beta_added"); u_scaled = sem("u_scaled"); u_turned = sem("u_turned")
        x2_ready = sem("x2_ready"); bias_added = sem("bias_added")
        l2_agg = sem("l2_agg"); l2_agg_copied = sem("l2_agg_copied"); l2_out = sem("l2_out")
        l2_normed = sem("l2_normed"); x3_ready = sem("x3_ready")
        l3_agg = sem("l3_agg"); l3_agg_copied = sem("l3_agg_copied"); l3_mid = sem("l3_mid")
        l3_relu = sem("l3_relu"); l3_out = sem("l3_out"); l3_biased = sem("l3_biased")
        l3_masked = sem("l3_masked"); x4_ready = sem("x4_ready")

        WEIGHT_LOADS = 17

        def wait_apart(eng, semaphore, count):
            eng.wait_ge(semaphore, count)
            eng.sem_inc(passed, 1)

        block = ctx.enter_context(nc.Block())

        @block.sync
        def _(sp):
            def column(v):
                return v.rearrange("(p o) -> p o", o=1)

            def everywhere(v):
                return v.rearrange("(o l) -> o l", o=1).broadcast_to([P, P])

            def load(n, c):
                sp.dma_start(chunk(X, n), x[bass.ds(n * NB, NB)].rearrange("b n f -> n b f")).then_inc(loaded[c], 16)
                sp.dma_start(ADJ[c][:], adj[bass.ds(n * NB, NB)].rearrange("b n f -> n b f")).then_inc(loaded[c], 16)

            def store_a(n, c):
                sp.wait_ge(a_part2, n + 1)
                sp.dma_start(a_scratch[bass.ds(n * NB, NB)].rearrange("b t i l -> i (b t) l"),
                             APART[c][:].rearrange("p b t l -> p (b t) l")).then_inc(a_stored[c], 16)

            for c in range(SLOTS):
                load(c, c)
                sp.sem_inc(a_stored[c], 16)
            for dst, src in ((W0, w0), (W1A, w1[0:P]), (W1B, w1[P:2 * P]), (W2, w2), (TH, theta),
                             (W31, w31), (W32, w32), (B0R, everywhere(b0)), (B2R, everywhere(b2)),
                             (BETAR, everywhere(beta)), (BIAS2R, everywhere(bias2)), (B32R, everywhere(b32)),
                             (B1, column(b1)), (B31, column(b31)), (GAM, column(gamma)),
                             (E3, eps3.rearrange("(o l) -> o l", o=1).broadcast_to([P, 1])), (MRAW, nodemask)):
                sp.dma_start(dst[:], src).then_inc(weights_in, 16)
            with sp.Fori(1, ROUNDS) as r:
                for c in range(SLOTS):
                    sp.wait_ge(adj_turned, r * SLOTS + (c + 1 - SLOTS))
                    sp.wait_ge(rowsum, r * SLOTS + (c + 1 - SLOTS))
                    load(r * SLOTS + c, c)
                for c in range(SLOTS):
                    store_a((r - 1) * SLOTS + c, c)
            for c in range(SLOTS):
                store_a((ROUNDS - 1) * SLOTS + c, c)
            for c in range(SLOTS):
                sp.wait_ge(a_stored[c], 16 * (ROUNDS + 1))

            def load_rows(b, slot):
                sp.dma_start(AROWS[0:PARTS * QUADS, slot, :],
                             a_scratch[b].rearrange("t (q s) l -> (t q) (s l)", s=QUAD)).then_inc(rows_in, 16)

            load_rows(0, 0)
            sp.wait_ge(rows_in, 16)
            load_rows(1, 1)
            with sp.Fori(1, GRAPHS // 2) as t:
                for k in range(2):
                    wait_apart(sp, rows_in, t * 32 + 16 * k)
                    wait_apart(sp, z_ready, t * (2 * GPG) + GPG * (k - 1))
                    load_rows(t * 2 + k, k)

            def reload(n, c):
                sp.dma_start(ADJ[c][:], adj[bass.ds(n * NB, NB)].rearrange("b n f -> n b f")).then_inc(reloaded[c], 16)

            def store_out(n, c):
                sp.wait_ge(x4_ready, n + 1)
                sp.dma_start(out[bass.ds(n * NB, NB)].rearrange("b n f -> n b f"), chunk(X, n)).then_inc(out_stored[c], 16)

            for c in range(SLOTS):
                reload(c, c)
            with sp.Fori(1, ROUNDS) as r:
                for c in range(SLOTS):
                    sp.wait_ge(l3_agg, r * SLOTS + (c + 1 - SLOTS))
                    reload(r * SLOTS + c, c)
                for c in range(SLOTS):
                    store_out((r - 1) * SLOTS + c, c)
            for c in range(SLOTS):
                store_out((ROUNDS - 1) * SLOTS + c, c)
            for c in range(SLOTS):
                sp.wait_ge(out_stored[c], 16 * ROUNDS)

        @block.gpsimd
        def _(pool):
            nc.gpsimd.memset(IDENT[:], 0.0).then_inc(const_step, 1)
            nc.gpsimd.memset(SEL[:], 0.0).then_inc(const_step, 1)
            nc.gpsimd.memset(AROWS[:], 0.0).then_inc(pool_const, 1)
            nc.gpsimd.memset(NHALF[:], -0.5).then_inc(pool_const, 1)
            nc.gpsimd.memset(EPSC[:], EPS).then_inc(pool_const, 1)
            pool.wait_ge(const_step, 2)
            nc.gpsimd.affine_select(out=IDENT[:], in_=IDENT[:], compare_op=ALU.not_equal, fill=1.0, base=0,
                                    pattern=[[-1, P]], channel_multiplier=1).then_inc(ident_ready, 1)
            for t in range(PARTS):
                pool.wait_ge(const_step, 2 + t)
                nc.gpsimd.affine_select(out=SEL[:], in_=SEL[:], compare_op=ALU.not_equal, fill=1.0, base=-QUADS * t,
                                        pattern=[[-1, QUADS], [0, P]], channel_multiplier=1).then_inc(const_step, 1)

            with pool.Fori(0, ROUNDS) as r:
                for c in range(SLOTS):
                    n = r * SLOTS + c
                    pool.wait_ge(a_part0, n + 1)
                    nc.gpsimd.tensor_tensor(AF[c][:], AF[c][:], APART[c][:, :, 0, :], ALU.subtract).then_inc(a_rest, 1)
                for c in range(SLOTS):
                    n = r * SLOTS + c
                    pool.wait_ge(a_part1, n + 1)
                    nc.gpsimd.tensor_tensor(APART[c][:, :, 2, :], AF[c][:], APART[c][:, :, 1, :],
                                            ALU.subtract).then_inc(a_part2, 1)

            pool.wait_ge(adjt_kept, CHUNKS)
            pool.wait_ge(pool_const, 3)
            def weights(g, k):
                s = slot(k)
                wait_apart(pool, var_ready, g + 1)
                nc.gpsimd.tensor_scalar(VE[:, s], VAR[:, s, :, 1], 1.0 / (SZ * SZ * SW * SW), EPS / (SW * SW),
                                        ALU.mult, ALU.add).then_inc(weight_step, 1)
                pool.wait_ge(weight_step, g * 2 + 1)
                nc.gpsimd.tensor_tensor(RSTD[:, s], VE[:, s], NHALF[:], ALU.pow).then_inc(weight_step, 1)
                pool.wait_ge(weight_step, g * 2 + 2)
                turned = ADJT[:, bass.ds(g * UG, UG)]
                nc.gpsimd.tensor_tensor(W32F[:, s], RSTD[:, s], turned, ALU.mult)
                nc.gpsimd.tensor_tensor(W16[:, s, :, 0], RSTD[:, s], turned, ALU.mult).then_inc(weight_high, 1)

            for k in range(-HEAD, 0):
                weights(HEAD + k, k)
            with pool.Fori(0, ITERS) as it:
                for k in range(BODY):
                    weights(group_at(it, k), k)

            pool.wait_ge(u_free, GROUPS // 2 + 2)
            with pool.Fori(0, ROUNDS) as r:
                for c in range(SLOTS):
                    n = r * SLOTS + c
                    if c == 0:
                        pool.wait_ge(rowsum, CHUNKS)
                    nc.gpsimd.tensor_tensor(T1[c][:], rows4(BETAR), cols4(S, n), ALU.mult).then_inc(beta_prod, 1)
                for c in range(SLOTS):
                    n = r * SLOTS + c
                    pool.wait_ge(beta_prod, n + 1)
                    nc.gpsimd.tensor_tensor(chunk(X, n), chunk(X, n), T1[c][:], ALU.add).then_inc(beta_added, 1)
                for c in range(SLOTS):
                    n = r * SLOTS + c
                    wait_apart(pool, ln[2].h, n + 1)
                    nc.gpsimd.tensor_tensor(chunk(X, n), chunk(X, n), rows4(BIAS2R), ALU.add).then_inc(bias_added, 1)
                pool.wait_ge(x4_ready, r * SLOTS + SLOTS)

        @block.scalar
        def _(act):
            def norm_std(L, c, n):
                act.wait_ge(L.var, n + 1)
                nc.scalar.activation(SD[c][:], MV[c][:, :, 1], ACT.Sqrt, bias=EPSC[:, 0:1]).then_inc(L.std, 1)

            def norm_relu(L, c, n, rs, nm, ready):
                wait_apart(act, ready, n + 1)
                for b in range(NB):
                    ins = nc.scalar.activation(H[c][:, b, :], X[:, bass.ds(n * CW + b * P, P)], ACT.Relu,
                                               bias=nm[c][:, b:b + 1], scale=rs[c][:, b:b + 1])
                ins.then_inc(L.h, 1)

            act.wait_ge(pool_const, 3)
            act.wait_ge(setup_done, 1)
            with act.Fori(0, ROUNDS) as r:
                for c in range(SLOTS):
                    n = r * SLOTS + c
                    act.wait_ge(adj_turned, n + 1)
                    nc.scalar.activation(chunk(ADJT, n), bank(c, 0), ACT.Copy).then_inc(adjt_kept, 1)
                for c in range(SLOTS):
                    norm_std(ln[0], c, r * SLOTS + c)
                for c in range(SLOTS):
                    norm_relu(ln[0], c, r * SLOTS + c, RS, NM, ln[0].scale)
                for c in range(SLOTS):
                    n = r * SLOTS + c
                    act.wait_ge(l0_agg, n + 1)
                    nc.scalar.activation(TT[c][:], bank(c, 1), ACT.Copy).then_inc(l0_agg_copied, 1)
                for c in range(SLOTS):
                    norm_std(ln[1], c, r * SLOTS + c)
                for c in range(SLOTS):
                    norm_relu(ln[1], c, r * SLOTS + c, RS, NM, ln[1].scale)
                for c in range(SLOTS):
                    n = r * SLOTS + c
                    act.wait_ge(h_turned, n + 1)
                    nc.scalar.activation(TT[c][:], bank(c, 1), ACT.Copy).then_inc(h_turned_copied, 1)
                for c in range(SLOTS):
                    n = r * SLOTS + c
                    act.wait_ge(ab_ready, n + 1)
                    act.wait_ge(a_stored[c], r * 16 + 16)
                    nc.scalar.activation(H[c][:], bank(c, 0), ACT.Identity, bias=NB1[:, 0:1], scale=-1.0)
                    nc.scalar.activation(chunk(NAT, n), bank(c, 0), ACT.Identity, bias=NB1[:, 0:1],
                                         scale=-1.0).then_inc(na_kept, 1)
                for c in range(SLOTS):
                    n = r * SLOTS + c
                    act.wait_ge(a_full, n + 1)
                    nc.scalar.activation(APART[c][:, :, 0, :], AF[c][:], ACT.Copy).then_inc(a_part0, 1)
                for c in range(SLOTS):
                    n = r * SLOTS + c
                    act.wait_ge(a_rest, n + 1)
                    nc.scalar.activation(APART[c][:, :, 1, :], AF[c][:], ACT.Copy).then_inc(a_part1, 1)

            for c in range(SLOTS):
                act.wait_ge(a_stored[c], 16 * (ROUNDS + 1))
            def split(g, k):
                s, z = slot(k), zslot(k)
                act.wait_ge(z_ready, g + 1)
                act.wait_ge(ring_free, g + 1)
                nc.scalar.activation(ZH[:, s].rearrange("p u l -> p (u l)"),
                                     PS[:, 2 * z:2 * z + 2, :].rearrange("p a l -> p (a l)"), ACT.Copy)
                for u in range(ACT_UNITS):
                    col = u % QUAD * P
                    ins = nc.scalar.activation(JUNK[:, s, u, :], PS[:, 2 * z + u // QUAD, col:col + P],
                                               ACT.Square, scale=float(P) ** -0.5, accum_out=VAR[:, s, u, 1:2])
                ins.then_inc(act_used, 1)

            for k in range(-HEAD, 0):
                split(HEAD + k, k)
            with act.Fori(0, ITERS) as it:
                for k in range(BODY):
                    split(group_at(it, k), k)

            act.wait_ge(deg_ready, 1)
            nc.scalar.activation(DSQ[:], DINV[:], ACT.Sqrt).then_inc(deg_root, 1)
            act.wait_ge(u_free, GROUPS // 2 + 2)
            with act.Fori(0, ROUNDS) as r:
                for c in range(SLOTS):
                    n = r * SLOTS + c
                    nc.scalar.activation(AF[c][:], chunk(NAT, n), ACT.Copy, scale=GAMS[:, 0:1]).then_inc(u_scaled, 1)
                for c in range(SLOTS):
                    norm_std(ln[2], c, r * SLOTS + c)
                for c in range(SLOTS):
                    norm_relu(ln[2], c, r * SLOTS + c, RSD, NMD, ln[2].scaled)
                for c in range(SLOTS):
                    n = r * SLOTS + c
                    act.wait_ge(l2_agg, n + 1)
                    nc.scalar.activation(TT[c][:], bank(c, 1), ACT.Copy).then_inc(l2_agg_copied, 1)
                for c in range(SLOTS):
                    norm_std(ln[3], c, r * SLOTS + c)
                for c in range(SLOTS):
                    norm_relu(ln[3], c, r * SLOTS + c, RS, NM, ln[3].scale)
                for c in range(SLOTS):
                    n = r * SLOTS + c
                    act.wait_ge(l3_agg, n + 1)
                    nc.scalar.activation(TT[c][:], bank(c, 1), ACT.Copy).then_inc(l3_agg_copied, 1)
                for c in range(SLOTS):
                    n = r * SLOTS + c
                    act.wait_ge(l3_mid, n + 1)
                    nc.scalar.activation(AF[c][:], bank(c, 0), ACT.Relu, bias=B31[:, 0:1]).then_inc(l3_relu, 1)
                act.wait_ge(l3_out, r * SLOTS + SLOTS)

        @block.vector
        def _(dve):
            def norm_stats(L, c, n):
                for b in range(NB):
                    ins = nc.vector.bn_stats(ST[c][:, b, :], X[:, bass.ds(n * CW + b * P, P)])
                ins.then_inc(L.stats, 1)

            def norm_var(L, c, n):
                wait_apart(dve, L.stats, n + 1)
                for b in range(NB):
                    ins = nc.vector.bn_aggr(MV[c][:, b, :], ST[c][:, b, :])
                ins.then_inc(L.var, 1)

            def norm_rstd(L, c, n):
                dve.wait_ge(L.std, n + 1)
                nc.vector.reciprocal(RS[c][:], SD[c][:]).then_inc(L.rstd, 1)

            def norm_shift(L, c, n):
                dve.wait_ge(L.rstd, n + 1)
                nc.vector.scalar_tensor_tensor(out=NM[c][:], in0=MV[c][:, :, 0], scalar=-1.0, in1=RS[c][:],
                                               op0=ALU.mult, op1=ALU.mult).then_inc(L.scale, 1)

            dve.wait_ge(weights_in, 16 * WEIGHT_LOADS)
            nc.vector.tensor_reduce(MEANS[:, 0:1], W2[:], AX.X, ALU.add)
            nc.vector.tensor_reduce(MEANS[:, 1:2], B2R[:], AX.X, ALU.add)
            nc.vector.tensor_scalar(NB1[:], B1[:], -1.0, None, ALU.mult)
            nc.vector.tensor_copy(MROW[:], MRAW[:])
            nc.vector.tensor_scalar(E3P1[:], E3[:], 1.0, None, ALU.add).then_inc(setup_step, 1)
            dve.wait_ge(setup_step, 1)
            nc.vector.tensor_scalar(MEANS[:, 2:4], MEANS[:, 0:2], 1.0 / P, None, ALU.mult).then_inc(setup_step, 1)
            dve.wait_ge(setup_step, 2)
            dve.wait_ge(ident_ready, 1)
            nc.vector.tensor_scalar(W2C[:], W2[:], MEANS[:, 2:3], SZ, ALU.subtract, ALU.mult)
            nc.vector.tensor_scalar(NW2C[:], W2[:], MEANS[:, 2:3], -SZ, ALU.subtract, ALU.mult)
            nc.vector.tensor_scalar(B2C[:], B2R[:], MEANS[:, 3:4], SZ, ALU.subtract, ALU.mult)
            nc.vector.tensor_scalar(GAMS[:], GAM[:], 1.0 / (SZ * SW), None, ALU.mult)
            nc.vector.tensor_scalar(DIAGE[:], IDENT[:], E3P1[:, 0:1], None, ALU.mult).then_inc(setup_done, 1)

            with dve.Fori(0, ROUNDS) as r:
                for c in range(SLOTS):
                    dve.wait_ge(loaded[c], r * 32 + 32)
                    norm_stats(ln[0], c, r * SLOTS + c)
                for c in range(SLOTS):
                    norm_var(ln[0], c, r * SLOTS + c)
                for c in range(SLOTS):
                    n = r * SLOTS + c
                    nc.vector.tensor_reduce(S[:, bass.ds(n * NB, NB)], ADJ[c][:], AX.X, ALU.add).then_inc(rowsum, 1)
                for c in range(SLOTS):
                    norm_rstd(ln[0], c, r * SLOTS + c)
                for c in range(SLOTS):
                    norm_shift(ln[0], c, r * SLOTS + c)
                for c in range(SLOTS):
                    n = r * SLOTS + c
                    dve.wait_ge(l0_out, n + 1)
                    nc.vector.tensor_tensor(T1[c][:], bank(c, 0), rows4(B0R), ALU.add).then_inc(l0_biased, 1)
                for c in range(SLOTS):
                    n = r * SLOTS + c
                    dve.wait_ge(l0_biased, n + 1)
                    nc.vector.scalar_tensor_tensor(out=chunk(X, n), in0=T1[c][:], scalar=0.0, in1=chunk(X, n),
                                                   op0=ALU.max, op1=ALU.add).then_inc(x1_ready, 1)
                for c in range(SLOTS):
                    wait_apart(dve, x1_ready, r * SLOTS + (c + 1))
                    norm_stats(ln[1], c, r * SLOTS + c)
                for c in range(SLOTS):
                    norm_var(ln[1], c, r * SLOTS + c)
                for c in range(SLOTS):
                    norm_rstd(ln[1], c, r * SLOTS + c)
                for c in range(SLOTS):
                    norm_shift(ln[1], c, r * SLOTS + c)
                for c in range(SLOTS):
                    n = r * SLOTS + c
                    dve.wait_ge(ab_ready, n + 1)
                    nc.vector.tensor_copy(chunk(BT, n), bank(c, 1)).then_inc(b_kept, 1)
                for c in range(SLOTS):
                    n = r * SLOTS + c
                    dve.wait_ge(a_prod, n + 1)
                    nc.vector.tensor_tensor(AF[c][:], bank(c, 0), rows4(B2C), ALU.add).then_inc(a_full, 1)

            def hidden(g, k):
                a = NAT[:, bass.ds(g * UG, UG)]
                b = BT[:, bass.ds(graph_of_group(g) * P, P)]
                nc.vector.tensor_tensor(HID[:, slot(k)],
                                        a.rearrange("p (u o) -> p u o", o=1).broadcast_to([P, UG, P]),
                                        b.rearrange("p (o j) -> p o j", o=1).broadcast_to([P, UG, P]),
                                        ALU.max).then_inc(hid_ready, 1)

            def keep_u(g, k):
                wait_apart(dve, ring_free, g + (2 + RING))
                nc.vector.tensor_reduce(NAT[:, bass.ds(g * UG, 2 * UG)],
                                        PS[:, pair_bank(k), 0:4 * UG].rearrange("p (i t) -> p i t", t=2),
                                        AX.X, ALU.add).then_inc(u_free, 1)

            def low_weights(g, k):
                s = slot(k)
                dve.wait_ge(weight_high, g + 1)
                nc.vector.tensor_tensor(W16[:, s, :, 1], W32F[:, s], W16[:, s, :, 0],
                                        ALU.subtract).then_inc(weight_ready, 1)

            def group(g, k, ahead):
                s, z = slot(k), zslot(k)
                dve.wait_ge(act_used, g + 1)
                for u in range(DVE_UNITS):
                    col = (ACT_UNITS + u) % QUAD * P
                    ins = nc.vector.bn_stats(STZ[:, s, u, :], PS[:, 2 * z + 1, col:col + P])
                ins.then_inc(bn_done, 1)
                nc.vector.tensor_tensor(ZL[:, s].rearrange("p u l -> p (u l)"),
                                        PS[:, 2 * z:2 * z + 2, :].rearrange("p a l -> p (a l)"),
                                        ZH[:, s].rearrange("p u l -> p (u l)"), ALU.subtract).then_inc(zl_ready, 1)
                wait_apart(dve, bn_done, g + 1)
                for u in range(DVE_UNITS):
                    ins = nc.vector.bn_aggr(VAR[:, s, ACT_UNITS + u, :], STZ[:, s, u, :])
                ins.then_inc(var_ready, 1)
                if ahead:
                    hidden(g + RING, k + RING)
                if HEAD + k >= 1:
                    low_weights(g - 1, k - 1)
                if k % 2 == 0 and HEAD + k >= 4:
                    keep_u(g - 4, k - 4)

            dve.sem_inc(u_free, 2)
            dve.wait_ge(na_kept, CHUNKS)
            dve.wait_ge(b_kept, CHUNKS)
            dve.wait_ge(a_prod, CHUNKS)
            dve.wait_ge(a_part2, CHUNKS)
            for g in range(RING):
                hidden(g, g - HEAD)
            for k in range(-HEAD, 0):
                group(HEAD + k, k, True)
            with dve.Fori(0, ITERS - 1) as it:
                for k in range(BODY):
                    group(group_at(it, k), k, True)
            for k in range(BODY):
                group(group_at(ITERS - 1, k), k, k + RING < BODY)
            low_weights(GROUPS - 1, BODY - 1)
            keep_u(GROUPS - 4, BODY - 4)
            keep_u(GROUPS - 2, BODY - 2)

            dve.wait_ge(rowsum, CHUNKS)
            nc.vector.tensor_scalar(DINV[:], S[:], 1.0, None, ALU.add).then_inc(deg_ready, 1)
            dve.wait_ge(deg_root, 1)
            nc.vector.reciprocal(DINV[:], DSQ[:]).then_inc(dinv_ready, 1)
            dve.wait_ge(mask_turned, 1)
            nc.vector.tensor_copy(MASK[:], PS[:, 7, 0:GRAPHS]).then_inc(setup_step, 1)
            with dve.Fori(0, ROUNDS) as r:
                for c in range(SLOTS):
                    n = r * SLOTS + c
                    dve.wait_ge(u_turned, n + 1)
                    dve.wait_ge(beta_added, n + 1)
                    nc.vector.tensor_tensor(chunk(X, n), chunk(X, n), bank(c, 0), ALU.add).then_inc(x2_ready, 1)
                for c in range(SLOTS):
                    wait_apart(dve, x2_ready, r * SLOTS + (c + 1))
                    norm_stats(ln[2], c, r * SLOTS + c)
                for c in range(SLOTS):
                    norm_var(ln[2], c, r * SLOTS + c)
                for c in range(SLOTS):
                    norm_rstd(ln[2], c, r * SLOTS + c)
                for c in range(SLOTS):
                    norm_shift(ln[2], c, r * SLOTS + c)
                for c in range(SLOTS):
                    n = r * SLOTS + c
                    dve.wait_ge(ln[2].scale, n + 1)
                    dve.wait_ge(dinv_ready, 1)
                    nc.vector.tensor_tensor(RSD[c][:], RS[c][:], DINV[:, bass.ds(n * NB, NB)], ALU.mult)
                    nc.vector.tensor_tensor(NMD[c][:], NM[c][:], DINV[:, bass.ds(n * NB, NB)],
                                            ALU.mult).then_inc(ln[2].scaled, 1)
                for c in range(SLOTS):
                    n = r * SLOTS + c
                    dve.wait_ge(l2_out, n + 1)
                    nc.vector.tensor_tensor(T1[c][:], bank(c, 0), cols4(DINV, n), ALU.mult).then_inc(l2_normed, 1)
                for c in range(SLOTS):
                    n = r * SLOTS + c
                    dve.wait_ge(l2_normed, n + 1)
                    dve.wait_ge(bias_added, n + 1)
                    nc.vector.tensor_tensor(chunk(X, n), T1[c][:], chunk(X, n), ALU.add).then_inc(x3_ready, 1)
                for c in range(SLOTS):
                    wait_apart(dve, x3_ready, r * SLOTS + (c + 1))
                    norm_stats(ln[3], c, r * SLOTS + c)
                for c in range(SLOTS):
                    norm_var(ln[3], c, r * SLOTS + c)
                for c in range(SLOTS):
                    norm_rstd(ln[3], c, r * SLOTS + c)
                for c in range(SLOTS):
                    norm_shift(ln[3], c, r * SLOTS + c)
                for c in range(SLOTS):
                    n = r * SLOTS + c
                    dve.wait_ge(l3_out, n + 1)
                    nc.vector.tensor_tensor(T1[c][:], bank(c, 1), rows4(B32R), ALU.add).then_inc(l3_biased, 1)
                for c in range(SLOTS):
                    n = r * SLOTS + c
                    dve.wait_ge(l3_biased, n + 1)
                    dve.wait_ge(setup_step, 3)
                    nc.vector.tensor_tensor(T1[c][:], T1[c][:], cols4(MASK, n), ALU.mult).then_inc(l3_masked, 1)
                for c in range(SLOTS):
                    n = r * SLOTS + c
                    dve.wait_ge(l3_masked, n + 1)
                    nc.vector.tensor_tensor(chunk(X, n), T1[c][:], chunk(X, n), ALU.add).then_inc(x4_ready, 1)

        @block.tensor
        def _(pe):
            def four(dst, c, lhs, rhs, *more):
                pairs = [(lhs, rhs), *more]
                for b in range(NB):
                    for k, (l, m) in enumerate(pairs):
                        ins = nc.tensor.matmul(dst[:, b, :], l(b), m(b), start=(k == 0), stop=(k == len(pairs) - 1))
                return ins

            def graph_of(t, n):
                return lambda b: t[:, bass.ds(n * CW + b * P, P)]

            pe.wait_ge(ident_ready, 1)
            pe.wait_ge(setup_done, 1)
            with pe.Fori(0, ROUNDS) as r:
                for c in range(SLOTS):
                    n = r * SLOTS + c
                    pe.wait_ge(loaded[c], r * 32 + 32)
                    for b in range(NB):
                        ins = nc.tensor.transpose(bank(c, 0)[:, b, :], ADJ[c][:, b, :], IDENT[:])
                    ins.then_inc(adj_turned, 1)
                for c in range(SLOTS):
                    n = r * SLOTS + c
                    pe.wait_ge(adjt_kept, n + 1)
                    pe.wait_ge(ln[0].h, n + 1)
                    four(bank(c, 1), c, lambda b: H[c][:, b, :], graph_of(ADJT, n)).then_inc(l0_agg, 1)
                for c in range(SLOTS):
                    n = r * SLOTS + c
                    pe.wait_ge(l0_agg_copied, n + 1)
                    four(bank(c, 0), c, lambda b: TT[c][:, b, :], lambda b: W0[:]).then_inc(l0_out, 1)
                for c in range(SLOTS):
                    n = r * SLOTS + c
                    pe.wait_ge(ln[1].h, n + 1)
                    for b in range(NB):
                        ins = nc.tensor.transpose(bank(c, 1)[:, b, :], H[c][:, b, :], IDENT[:])
                    ins.then_inc(h_turned, 1)
                for c in range(SLOTS):
                    n = r * SLOTS + c
                    pe.wait_ge(h_turned_copied, n + 1)
                    ht = TT[c][:].rearrange("p b l -> p (b l)")
                    nc.tensor.matmul(PS[:, 2 * c, :], W1A[:], ht, start=True, stop=True)
                    nc.tensor.matmul(PS[:, 2 * c + 1, :], W1B[:], ht, start=True, stop=True).then_inc(ab_ready, 1)
                for c in range(SLOTS):
                    n = r * SLOTS + c
                    pe.wait_ge(na_kept, n + 1)
                    for b in range(NB):
                        ins = nc.tensor.matmul(bank(c, 0)[:, b, :], H[c][:, b, :], NW2C[:], start=True, stop=True)
                    ins.then_inc(a_prod, 1)
                pe.wait_ge(b_kept, r * SLOTS + SLOTS)
                pe.wait_ge(a_full, r * SLOTS + SLOTS)

            def product(g, k):
                s, z = slot(k), zslot(k)
                graph = graph_of_group(g)
                pe.wait_ge(rows_in, graph * 16 + 16)
                if not (isinstance(g, int) and g < ZRING):
                    pe.wait_ge(zl_ready, g + (1 - ZRING))
                for q in range(2):
                    nc.tensor.matmul(PS[:, 2 * z + q, :],
                                     SEL[:, bass.ds((g & (GPG - 1)) * 2 + q, 1), :].rearrange("p o j -> p (o j)"),
                                     AROWS[:, bass.ds(graph & 1, 1), :].rearrange("p o l -> p (o l)"),
                                     start=True, stop=False, skip_group_check=True)
                pe.wait_ge(hid_ready, g + 1)
                for u in range(UG):
                    col = u % QUAD * P
                    ins = nc.tensor.matmul(PS[:, 2 * z + u // QUAD, col:col + P], HID[:, s, u, :], W2C[:],
                                           start=False, stop=(u % QUAD == QUAD - 1), skip_group_check=True)
                ins.then_inc(z_ready, 1)

            def weighted_sum(g, k):
                s = slot(k)
                pe.wait_ge(weight_ready, g + 1)
                pe.wait_ge(zl_ready, g + 1)
                if k % 2 == 0:
                    pe.wait_ge(u_free, (g >> 1) + 1)
                for u in range(UG):
                    col = 2 * (k % 2 * UG + u)
                    nc.tensor.matmul(PS[:, pair_bank(k), col:col + 2], ZH[:, s, u, :], W16[:, s, u, :],
                                     start=True, stop=False, skip_group_check=True)
                    ins = nc.tensor.matmul(PS[:, pair_bank(k), col:col + 1], ZL[:, s, u, :], W16[:, s, u, 0:1],
                                           start=False, stop=True, skip_group_check=True)
                ins.then_inc(ring_free, 1)

            pe.wait_ge(pool_const, 3)
            pe.wait_ge(const_step, 2 + PARTS)
            pe.sem_inc(ring_free, RING)
            for k in range(-HEAD, 0):
                product(HEAD + k, k)
            for k in range(-HEAD, 0):
                product(HEAD + k + RING, k + RING)
                weighted_sum(HEAD + k, k)
            with pe.Fori(0, ITERS - 1) as it:
                for k in range(BODY):
                    product(group_at(it, k + RING), k + RING)
                    weighted_sum(group_at(it, k), k)
            for k in range(BODY):
                if k + RING < BODY:
                    product(group_at(ITERS - 1, k + RING), k + RING)
                weighted_sum(group_at(ITERS - 1, k), k)

            pe.wait_ge(zl_ready, GROUPS)
            pe.wait_ge(u_free, GROUPS // 2 + 2)
            nc.tensor.transpose(PS[:, 7, 0:GRAPHS], MROW[:], IDENT[0:GRAPHS, 0:GRAPHS]).then_inc(mask_turned, 1)
            pe.wait_ge(setup_step, 3)
            with pe.Fori(0, ROUNDS) as r:
                for c in range(SLOTS):
                    n = r * SLOTS + c
                    pe.wait_ge(u_scaled, n + 1)
                    for b in range(NB):
                        ins = nc.tensor.transpose(bank(c, 0)[:, b, :], AF[c][:, b, :], IDENT[:])
                    ins.then_inc(u_turned, 1)
                for c in range(SLOTS):
                    n = r * SLOTS + c
                    pe.wait_ge(ln[2].h, n + 1)
                    four(bank(c, 1), c, lambda b: H[c][:, b, :], graph_of(ADJT, n),
                         (lambda b: H[c][:, b, :], lambda b: IDENT[:])).then_inc(l2_agg, 1)
                for c in range(SLOTS):
                    n = r * SLOTS + c
                    pe.wait_ge(l2_agg_copied, n + 1)
                    four(bank(c, 0), c, lambda b: TT[c][:, b, :], lambda b: TH[:]).then_inc(l2_out, 1)
                for c in range(SLOTS):
                    n = r * SLOTS + c
                    pe.wait_ge(ln[3].h, n + 1)
                    pe.wait_ge(reloaded[c], r * 16 + 16)
                    four(bank(c, 1), c, lambda b: H[c][:, b, :], lambda b: ADJ[c][:, b, :],
                         (lambda b: H[c][:, b, :], lambda b: DIAGE[:])).then_inc(l3_agg, 1)
                for c in range(SLOTS):
                    n = r * SLOTS + c
                    pe.wait_ge(l3_agg_copied, n + 1)
                    nc.tensor.matmul(PS[:, 2 * c, :], W31[:], TT[c][:].rearrange("p b l -> p (b l)"),
                                     start=True, stop=True).then_inc(l3_mid, 1)
                for c in range(SLOTS):
                    n = r * SLOTS + c
                    pe.wait_ge(l3_relu, n + 1)
                    four(bank(c, 1), c, lambda b: AF[c][:, b, :], lambda b: W32[:]).then_inc(l3_out, 1)
                pe.wait_ge(l3_biased, r * SLOTS + SLOTS)


_ARGS = ["x", "adj", "nodemask", "L0_gnn_W", "L0_gnn_b", "L1_gnn_W1", "L1_gnn_b1", "L1_gnn_W2", "L1_gnn_b2",
         "L1_gnn_gamma", "L1_gnn_beta", "L2_gnn_theta", "L2_gnn_bias", "L3_gnn_W1", "L3_gnn_b1", "L3_gnn_W2",
         "L3_gnn_b2", "L3_gnn_eps"]


def kernel(**inputs):
    import numpy as _np
    import concourse.bacc as _bacc
    from concourse import mybir as _mybir
    from concourse.bass_utils import run_bass_kernel_spmd as _run

    nc = _bacc.Bacc("TRN2", target_bir_lowering=False, num_devices=1)
    arrays, args = {}, []
    for name in _ARGS:
        a = _np.ascontiguousarray(inputs[name])
        if a.dtype == _np.bool_:
            a = a.view(_np.uint8)
        arrays[f"in_{name}"] = a
        args.append(nc.dram_tensor(f"in_{name}", a.shape, _mybir.dt.from_np(a.dtype), kind="ExternalInput").ap())
    out = nc.dram_tensor("out_x", (GRAPHS, P, P), F32, kind="ExternalOutput").ap()
    gnn_stack(nc, *args, out)
    r = _run(nc, [arrays], core_ids=[0])
    return r.results[0]["out_x"]
```

```python
from contextlib import ExitStack

import concourse.bass as bass
from concourse import mybir

F32 = mybir.dt.float32
BF16 = mybir.dt.bfloat16
F16 = mybir.dt.float16
U8 = mybir.dt.uint8
ALU = mybir.AluOpType
ACT = mybir.ActivationFunctionType
AX = mybir.AxisListType

P = 128
GRAPHS = 64
EPS = 1e-5
NB = 4
CW = NB * P
SLOTS = 4
ROUNDS = GRAPHS // (NB * SLOTS)
CHUNKS = GRAPHS // NB

UG = 8
GW = UG * P
GROUPS = GRAPHS * P // UG
RING = 4
ZRING = 3
BODY = RING * ZRING
HEAD = GROUPS % BODY
ITERS = (GROUPS - HEAD) // BODY
assert HEAD == RING
GPG = P // UG
QUAD = 4
QUADS = P // QUAD
PARTS = 3
DVE_UNITS = 1
ACT_UNITS = UG - DVE_UNITS
SZ = 64.0
SW = 64.0


def gnn_stack(nc, x, adj, nodemask, w0, b0, w1, b1, w2, b2, gamma, beta, theta, bias2,
              w31, b31, w32, b32, eps3, out):
    a_scratch = nc.dram_tensor("a_scratch", [GRAPHS, PARTS, P, P], BF16, kind="Internal").ap()

    with ExitStack() as ctx:
        def sb(name, shape, dt=F32):
            return ctx.enter_context(nc.sbuf_tensor(name, shape, dt))

        def sem(name):
            return ctx.enter_context(nc.semaphore(name))

        X = sb("X", [P, GRAPHS * P])
        ADJT = sb("ADJT", [P, GRAPHS * P])
        NAT = sb("NAT", [P, GRAPHS * P])
        BT = sb("BT", [P, GRAPHS * P])
        S = sb("S", [P, GRAPHS])
        DINV = sb("DINV", [P, GRAPHS])
        DSQ = sb("DSQ", [P, GRAPHS])
        MASK = sb("MASK", [P, GRAPHS])

        W0 = sb("W0", [P, P]); W1A = sb("W1A", [P, P]); W1B = sb("W1B", [P, P]); W2 = sb("W2", [P, P])
        W2C = sb("W2C", [P, P])
        NW2C = sb("NW2C", [P, P])
        TH = sb("TH", [P, P]); W31 = sb("W31", [P, P]); W32 = sb("W32", [P, P])
        B0R = sb("B0R", [P, P]); B2R = sb("B2R", [P, P]); BETAR = sb("BETAR", [P, P])
        BIAS2R = sb("BIAS2R", [P, P]); B32R = sb("B32R", [P, P])
        B2C = sb("B2C", [P, P])
        B1 = sb("B1", [P, 1]); NB1 = sb("NB1", [P, 1]); B31 = sb("B31", [P, 1])
        GAM = sb("GAM", [P, 1]); E3 = sb("E3", [P, 1]); E3P1 = sb("E3P1", [P, 1]); EPSC = sb("EPSC", [P, 1])
        MEANS = sb("MEANS", [P, 4])
        IDENT = sb("IDENT", [P, P])
        GAMS = sb("GAMS", [P, 1])
        DIAGE = sb("DIAGE", [P, P])
        NHALF = sb("NHALF", [P, UG])
        MRAW = sb("MRAW", [GRAPHS, P], U8); MROW = sb("MROW", [GRAPHS, P])
        SEL = sb("SEL", [P, QUADS, P], BF16)

        RINGS = 4 * SLOTS * CW
        assert 2 * RING * GW == RINGS
        ARENA = sb("ARENA", [P, RINGS + SLOTS * CW + SLOTS * CW * PARTS // 2])

        def share(first, words, dt=F32):
            t = ARENA[:, first:first + words]
            return t if dt == F32 else t.bitcast(dt)

        H, TT, T1, AF = ([share((k * SLOTS + c) * CW, CW).rearrange("p (b l) -> p b l", b=NB) for c in range(SLOTS)]
                         for k in range(4))
        ADJ = [share(RINGS + c * CW, CW).rearrange("p (b l) -> p b l", b=NB) for c in range(SLOTS)]
        APART = [share(RINGS + SLOTS * CW + c * CW * PARTS // 2, CW * PARTS // 2, BF16)
                 .rearrange("p (b t l) -> p b t l", b=NB, t=PARTS) for c in range(SLOTS)]

        def slots(name, shape):
            return [sb(f"{name}{c}", shape) for c in range(SLOTS)]
        ST = slots("ST", [P, NB, 6]); MV = slots("MV", [P, NB, 2])
        SD = slots("SD", [P, NB]); RS = slots("RS", [P, NB]); NM = slots("NM", [P, NB])
        RSD = slots("RSD", [P, NB]); NMD = slots("NMD", [P, NB])

        HID = share(0, RING * GW).rearrange("p (r u j) -> p r u j", r=RING, u=UG)
        ZH = share(RING * GW, RING * GW // 2, F16).rearrange("p (r u l) -> p r u l", r=RING, u=UG)
        ZL = share(RING * GW * 3 // 2, RING * GW // 2, F16).rearrange("p (r u l) -> p r u l", r=RING, u=UG)
        JUNK = share(RINGS + SLOTS * CW, RING * ACT_UNITS * P // 2, BF16).rearrange("p (r u l) -> p r u l", r=RING, u=ACT_UNITS)
        AROWS = sb("AROWS", [P, 2, QUAD * P], BF16)
        STZ = sb("STZ", [P, RING, DVE_UNITS, 6])
        VAR = sb("VAR", [P, RING, UG, 2])
        VE = sb("VE", [P, RING, UG]); RSTD = sb("RSTD", [P, RING, UG]); W32F = sb("W32F", [P, RING, UG])
        W16 = sb("W16", [P, RING, UG, 2], F16)

        PS = ctx.enter_context(nc.psum_tensor("PS", [P, 8, 512], F32))

        def bank(c, k):
            return PS[:, 2 * c + k, :].rearrange("p (b l) -> p b l", b=NB)

        def on(stage, r, q, age):
            k = r + (q - age) // SLOTS
            if not isinstance(r, int) or 0 <= k < ROUNDS:
                stage(r * SLOTS + (q - age), (q - age) % SLOTS, k)

        def all_steps(eng, step):
            for q in range(SLOTS):
                step(0, q)
            with eng.Fori(1, ROUNDS) as r:
                for q in range(SLOTS):
                    step(r, q)
            for q in range(SLOTS):
                step(ROUNDS, q)

        def chunk(t, n):
            return t[:, bass.ds(n * CW, CW)].rearrange("p (b l) -> p b l", b=NB)

        def group_at(it, k):
            return it * BODY + (HEAD + k)

        def slot(k):
            return (HEAD + k) % RING

        def zslot(k):
            return (HEAD + k) % ZRING

        def pair_bank(k):
            return 6 + k // 2 % 2

        def graph_of_group(g):
            if isinstance(g, int):
                return g // GPG
            return nc.s_assert_within(g >> (GPG.bit_length() - 1), 0, GRAPHS - 1,
                                      skip_runtime_bounds_check_because="g is below GROUPS")

        def rows4(t):
            return t[:, :].rearrange("p (o l) -> p o l", o=1).broadcast_to([P, NB, P])

        def cols4(t, n):
            return t[:, bass.ds(n * NB, NB)].rearrange("p (b o) -> p b o", o=1).broadcast_to([P, NB, P])

        weights_in = sem("weights_in"); passed = sem("passed")
        const_step = sem("const_step"); pool_const = sem("pool_const"); ident_ready = sem("ident_ready")
        setup_step = sem("setup_step"); setup_done = sem("setup_done")
        mask_turned = sem("mask_turned")
        loaded = [sem(f"loaded{c}") for c in range(SLOTS)]
        reloaded = [sem(f"reloaded{c}") for c in range(SLOTS)]
        a_stored = [sem(f"a_stored{c}") for c in range(SLOTS)]
        out_stored = [sem(f"out_stored{c}") for c in range(SLOTS)]

        class Norm:
            def __init__(self, n):
                self.stats, self.var, self.std, self.rstd, self.scale, self.scaled, self.h = (
                    sem(f"ln{n}_{s}") for s in ("stats", "var", "std", "rstd", "scale", "scaled", "h"))
        ln = [Norm(n) for n in range(4)]

        adj_turned = sem("adj_turned"); adjt_kept = sem("adjt_kept"); rowsum = sem("rowsum")
        l0_agg = sem("l0_agg"); l0_agg_copied = sem("l0_agg_copied"); l0_out = sem("l0_out")
        l0_biased = sem("l0_biased"); x1_ready = sem("x1_ready")
        h_turned = sem("h_turned"); h_turned_copied = sem("h_turned_copied")
        ab_ready = sem("ab_ready"); na_kept = sem("na_kept"); b_kept = sem("b_kept")
        a_prod = sem("a_prod"); a_full = sem("a_full"); a_part0 = sem("a_part0")
        a_rest = sem("a_rest"); a_part1 = sem("a_part1"); a_part2 = sem("a_part2")

        rows_in = sem("rows_in"); hid_ready = sem("hid_ready"); z_ready = sem("z_ready")
        zl_ready = sem("zl_ready")
        act_used = sem("act_used")
        bn_done = sem("bn_done"); var_ready = sem("var_ready")
        weight_step = sem("weight_step"); weight_high = sem("weight_high"); weight_ready = sem("weight_ready")
        ring_free = sem("ring_free"); u_free = sem("u_free")

        deg_ready = sem("deg_ready"); deg_root = sem("deg_root"); dinv_ready = sem("dinv_ready")
        beta_prod = sem("beta_prod"); beta_added = sem("beta_added"); u_scaled = sem("u_scaled"); u_turned = sem("u_turned")
        x2_ready = sem("x2_ready"); bias_added = sem("bias_added")
        l2_agg = sem("l2_agg"); l2_agg_copied = sem("l2_agg_copied"); l2_out = sem("l2_out")
        l2_normed = sem("l2_normed"); x3_ready = sem("x3_ready")
        l3_agg = sem("l3_agg"); l3_agg_copied = sem("l3_agg_copied"); l3_mid = sem("l3_mid")
        l3_relu = sem("l3_relu"); l3_out = sem("l3_out"); l3_biased = sem("l3_biased")
        l3_masked = sem("l3_masked"); x4_ready = sem("x4_ready")

        WEIGHT_LOADS = 17

        def wait_apart(eng, semaphore, count):
            eng.wait_ge(semaphore, count)
            eng.sem_inc(passed, 1)

        block = ctx.enter_context(nc.Block())

        @block.sync
        def _(sp):
            def column(v):
                return v.rearrange("(p o) -> p o", o=1)

            def everywhere(v):
                return v.rearrange("(o l) -> o l", o=1).broadcast_to([P, P])

            def load(n, c):
                sp.dma_start(chunk(X, n), x[bass.ds(n * NB, NB)].rearrange("b n f -> n b f")).then_inc(loaded[c], 16)
                sp.dma_start(ADJ[c][:], adj[bass.ds(n * NB, NB)].rearrange("b n f -> n b f")).then_inc(loaded[c], 16)

            def store_a(n, c):
                sp.wait_ge(a_part2, n + 1)
                sp.dma_start(a_scratch[bass.ds(n * NB, NB)].rearrange("b t i l -> i (b t) l"),
                             APART[c][:].rearrange("p b t l -> p (b t) l")).then_inc(a_stored[c], 16)

            load(0, 0)
            for dst, src in ((W0, w0), (W1A, w1[0:P]), (W1B, w1[P:2 * P]), (W2, w2), (TH, theta),
                             (W31, w31), (W32, w32), (B0R, everywhere(b0)), (B2R, everywhere(b2)),
                             (BETAR, everywhere(beta)), (BIAS2R, everywhere(bias2)), (B32R, everywhere(b32)),
                             (B1, column(b1)), (B31, column(b31)), (GAM, column(gamma)),
                             (E3, eps3.rearrange("(o l) -> o l", o=1).broadcast_to([P, 1])), (MRAW, nodemask)):
                sp.dma_start(dst[:], src).then_inc(weights_in, 16)
            for c in range(1, SLOTS):
                load(c, c)
            for c in range(SLOTS):
                sp.sem_inc(a_stored[c], 16)
            with sp.Fori(1, ROUNDS) as r:
                for c in range(SLOTS):
                    sp.wait_ge(adj_turned, r * SLOTS + (c + 1 - SLOTS))
                    sp.wait_ge(rowsum, r * SLOTS + (c + 1 - SLOTS))
                    load(r * SLOTS + c, c)
                    store_a((r - 1) * SLOTS + c, c)

            def load_rows(b, half):
                sp.dma_start(AROWS[0:PARTS * QUADS, half, :],
                             a_scratch[b].rearrange("t (q s) l -> (t q) (s l)", s=QUAD)).then_inc(rows_in, 16)

            sp.wait_ge(a_stored[0], 16 * ROUNDS)
            load_rows(0, 0)
            sp.wait_ge(rows_in, 16)
            load_rows(1, 1)
            for c in range(SLOTS):
                store_a((ROUNDS - 1) * SLOTS + c, c)
            for c in range(SLOTS):
                sp.wait_ge(a_stored[c], 16 * (ROUNDS + 1))

            with sp.Fori(1, GRAPHS // 2) as t:
                for k in range(2):
                    wait_apart(sp, rows_in, t * 32 + 16 * k)
                    wait_apart(sp, z_ready, t * (2 * GPG) + GPG * (k - 1))
                    load_rows(t * 2 + k, k)

            def reload(n, c):
                sp.dma_start(ADJ[c][:], adj[bass.ds(n * NB, NB)].rearrange("b n f -> n b f")).then_inc(reloaded[c], 16)

            def store_out(n, c):
                sp.wait_ge(x4_ready, n + 1)
                sp.dma_start(out[bass.ds(n * NB, NB)].rearrange("b n f -> n b f"), chunk(X, n)).then_inc(out_stored[c], 16)

            for c in range(SLOTS):
                reload(c, c)
            with sp.Fori(1, ROUNDS) as r:
                for c in range(SLOTS):
                    sp.wait_ge(l3_agg, r * SLOTS + (c + 1 - SLOTS))
                    reload(r * SLOTS + c, c)
                    store_out((r - 1) * SLOTS + c, c)
            for c in range(SLOTS):
                store_out((ROUNDS - 1) * SLOTS + c, c)
            for c in range(SLOTS):
                sp.wait_ge(out_stored[c], 16 * ROUNDS)

        @block.gpsimd
        def _(pool):
            nc.gpsimd.memset(IDENT[:], 0.0).then_inc(const_step, 1)
            nc.gpsimd.memset(SEL[:], 0.0).then_inc(const_step, 1)
            nc.gpsimd.memset(AROWS[:], 0.0).then_inc(pool_const, 1)
            nc.gpsimd.memset(NHALF[:], -0.5).then_inc(pool_const, 1)
            nc.gpsimd.memset(EPSC[:], EPS).then_inc(pool_const, 1)
            pool.wait_ge(const_step, 2)
            nc.gpsimd.affine_select(out=IDENT[:], in_=IDENT[:], compare_op=ALU.not_equal, fill=1.0, base=0,
                                    pattern=[[-1, P]], channel_multiplier=1).then_inc(ident_ready, 1)
            for t in range(PARTS):
                pool.wait_ge(const_step, 2 + t)
                nc.gpsimd.affine_select(out=SEL[:], in_=SEL[:], compare_op=ALU.not_equal, fill=1.0, base=-QUADS * t,
                                        pattern=[[-1, QUADS], [0, P]], channel_multiplier=1).then_inc(const_step, 1)

            pool.sem_inc(beta_added, SLOTS)

            def first_rest(n, c, k):
                pool.wait_ge(a_part0, n + 1)
                nc.gpsimd.tensor_tensor(AF[c][:], AF[c][:], APART[c][:, :, 0, :], ALU.subtract).then_inc(a_rest, 1)

            def third_part(n, c, k):
                pool.wait_ge(a_part1, n + 1)
                nc.gpsimd.tensor_tensor(APART[c][:, :, 2, :], AF[c][:], APART[c][:, :, 1, :],
                                        ALU.subtract).then_inc(a_part2, 1)

            def beta_term(n, c, k):
                wait_apart(pool, ln[1].h, n + 1)
                nc.gpsimd.tensor_tensor(T1[c][:], rows4(BETAR), cols4(S, n), ALU.mult).then_inc(beta_prod, 1)

            def beta_add(n, c, k):
                wait_apart(pool, beta_prod, n + 1)
                nc.gpsimd.tensor_tensor(chunk(X, n), chunk(X, n), T1[c][:], ALU.add).then_inc(beta_added, 1)

            def step1(r, q):
                on(first_rest, r, q, 4)
                on(third_part, r, q, 4)
                on(beta_term, r, q, 3)
                on(beta_add, r, q, 3)

            pool.wait_ge(weights_in, 16 * WEIGHT_LOADS)
            all_steps(pool, step1)

            pool.wait_ge(adjt_kept, CHUNKS)
            pool.wait_ge(pool_const, 3)

            def weights(g, k):
                s = slot(k)
                wait_apart(pool, var_ready, g + 1)
                nc.gpsimd.tensor_scalar(VE[:, s], VAR[:, s, :, 1], 1.0 / (SZ * SZ * SW * SW), EPS / (SW * SW),
                                        ALU.mult, ALU.add).then_inc(weight_step, 1)
                pool.wait_ge(weight_step, g * 2 + 1)
                nc.gpsimd.tensor_tensor(RSTD[:, s], VE[:, s], NHALF[:], ALU.pow).then_inc(weight_step, 1)
                pool.wait_ge(weight_step, g * 2 + 2)
                turned = ADJT[:, bass.ds(g * UG, UG)]
                nc.gpsimd.tensor_tensor(W32F[:, s], RSTD[:, s], turned, ALU.mult)
                nc.gpsimd.tensor_tensor(W16[:, s, :, 0], RSTD[:, s], turned, ALU.mult).then_inc(weight_high, 1)

            for k in range(-HEAD, 0):
                weights(HEAD + k, k)
            with pool.Fori(0, ITERS) as it:
                for k in range(BODY):
                    weights(group_at(it, k), k)

            def add_bias2(n, c, k):
                wait_apart(pool, ln[2].h, n + 1)
                nc.gpsimd.tensor_tensor(chunk(X, n), chunk(X, n), rows4(BIAS2R), ALU.add).then_inc(bias_added, 1)

            all_steps(pool, lambda r, q: on(add_bias2, r, q, 0))

        @block.scalar
        def _(act):
            def norm_std(L, n, c):
                act.wait_ge(L.var, n + 1)
                nc.scalar.activation(SD[c][:], MV[c][:, :, 1], ACT.Sqrt, bias=EPSC[:, 0:1]).then_inc(L.std, 1)

            def norm_relu(L, n, c, rs, nm, ready):
                wait_apart(act, ready, n + 1)
                for b in range(NB):
                    ins = nc.scalar.activation(H[c][:, b, :], X[:, bass.ds(n * CW + b * P, P)], ACT.Relu,
                                               bias=nm[c][:, b:b + 1], scale=rs[c][:, b:b + 1])
                ins.then_inc(L.h, 1)

            act.wait_ge(pool_const, 3)

            def keep_adjt(n, c, k):
                act.wait_ge(adj_turned, n + 1)
                nc.scalar.activation(chunk(ADJT, n), bank(c, 0), ACT.Copy).then_inc(adjt_kept, 1)

            def copy_agg0(n, c, k):
                act.wait_ge(l0_agg, n + 1)
                nc.scalar.activation(TT[c][:], bank(c, 1), ACT.Copy).then_inc(l0_agg_copied, 1)

            def copy_h(n, c, k):
                act.wait_ge(h_turned, n + 1)
                nc.scalar.activation(TT[c][:], bank(c, 1), ACT.Copy).then_inc(h_turned_copied, 1)

            def keep_na(n, c, k):
                act.wait_ge(ab_ready, n + 1)
                act.wait_ge(a_stored[c], k * 16 + 16)
                nc.scalar.activation(H[c][:], bank(c, 0), ACT.Identity, bias=NB1[:, 0:1], scale=-1.0)
                nc.scalar.activation(chunk(NAT, n), bank(c, 0), ACT.Identity, bias=NB1[:, 0:1],
                                     scale=-1.0).then_inc(na_kept, 1)

            def part0(n, c, k):
                act.wait_ge(a_full, n + (1 + SLOTS))
                nc.scalar.activation(APART[c][:, :, 0, :], AF[c][:], ACT.Copy).then_inc(a_part0, 1)

            def part1(n, c, k):
                act.wait_ge(a_rest, n + 1)
                nc.scalar.activation(APART[c][:, :, 1, :], AF[c][:], ACT.Copy).then_inc(a_part1, 1)

            def step1(r, q):
                if isinstance(r, int) and (r, q) == (0, 1):
                    act.wait_ge(setup_done, 1)
                on(keep_adjt, r, q, 0)
                on(lambda n, c, k: norm_std(ln[1], n, c), r, q, 2)
                on(keep_na, r, q, 3)
                on(copy_agg0, r, q, 1)
                on(lambda n, c, k: norm_relu(ln[1], n, c, RS, NM, ln[1].scale), r, q, 2)
                on(lambda n, c, k: norm_std(ln[0], n, c), r, q, 0)
                on(part0, r, q, 3)
                on(copy_h, r, q, 2)
                on(lambda n, c, k: norm_relu(ln[0], n, c, RS, NM, ln[0].scale), r, q, 0)
                on(part1, r, q, 3)

            all_steps(act, step1)

            for c in range(SLOTS):
                act.wait_ge(a_stored[c], 16 * (ROUNDS + 1))
            act.wait_ge(beta_added, CHUNKS + SLOTS)

            def high_part(g, k):
                s, z = slot(k), zslot(k)
                act.wait_ge(z_ready, g + 1)
                act.wait_ge(ring_free, g + 1)
                nc.scalar.activation(ZH[:, s].rearrange("p u l -> p (u l)"),
                                     PS[:, 2 * z:2 * z + 2, :].rearrange("p a l -> p (a l)"), ACT.Copy)
                for u in range(ACT_UNITS):
                    col = u % QUAD * P
                    ins = nc.scalar.activation(JUNK[:, s, u, :], PS[:, 2 * z + u // QUAD, col:col + P],
                                               ACT.Square, scale=float(P) ** -0.5, accum_out=VAR[:, s, u, 1:2])
                ins.then_inc(act_used, 1)

            for k in range(-HEAD, 0):
                high_part(HEAD + k, k)
            with act.Fori(0, ITERS) as it:
                for k in range(BODY):
                    high_part(group_at(it, k), k)

            act.wait_ge(deg_ready, 1)
            nc.scalar.activation(DSQ[:], DINV[:], ACT.Sqrt).then_inc(deg_root, 1)
            act.wait_ge(u_free, GROUPS // 2 + 2)

            def scale_u(n, c, k):
                nc.scalar.activation(H[c][:], chunk(NAT, n), ACT.Copy, scale=GAMS[:, 0:1]).then_inc(u_scaled, 1)

            def copy_agg2(n, c, k):
                act.wait_ge(l2_agg, n + 1)
                nc.scalar.activation(TT[c][:], bank(c, 1), ACT.Copy).then_inc(l2_agg_copied, 1)

            def copy_agg3(n, c, k):
                act.wait_ge(l3_agg, n + 1)
                nc.scalar.activation(TT[c][:], bank(c, 1), ACT.Copy).then_inc(l3_agg_copied, 1)

            def relu_mid(n, c, k):
                act.wait_ge(l3_mid, n + 1)
                nc.scalar.activation(AF[c][:], bank(c, 0), ACT.Relu, bias=B31[:, 0:1]).then_inc(l3_relu, 1)

            def step3(r, q):
                on(copy_agg2, r, q, 2)
                on(lambda n, c, k: norm_std(ln[2], n, c), r, q, 1)
                on(relu_mid, r, q, 4)
                on(scale_u, r, q, 0)
                on(lambda n, c, k: norm_relu(ln[3], n, c, RS, NM, ln[3].scale), r, q, 3)
                on(lambda n, c, k: norm_relu(ln[2], n, c, RSD, NMD, ln[2].scaled), r, q, 1)
                on(copy_agg3, r, q, 3)
                on(lambda n, c, k: norm_std(ln[3], n, c), r, q, 2)

            all_steps(act, step3)

        @block.vector
        def _(dve):
            def norm_stats(L, n, c):
                for b in range(NB):
                    ins = nc.vector.bn_stats(ST[c][:, b, :], X[:, bass.ds(n * CW + b * P, P)])
                ins.then_inc(L.stats, 1)

            def norm_var(L, n, c):
                wait_apart(dve, L.stats, n + 1)
                for b in range(NB):
                    ins = nc.vector.bn_aggr(MV[c][:, b, :], ST[c][:, b, :])
                ins.then_inc(L.var, 1)

            def norm_rstd(L, n, c):
                dve.wait_ge(L.std, n + 1)
                nc.vector.reciprocal(RS[c][:], SD[c][:]).then_inc(L.rstd, 1)

            def norm_shift(L, n, c):
                dve.wait_ge(L.rstd, n + 1)
                nc.vector.scalar_tensor_tensor(out=NM[c][:], in0=MV[c][:, :, 0], scalar=-1.0, in1=RS[c][:],
                                               op0=ALU.mult, op1=ALU.mult).then_inc(L.scale, 1)

            dve.sem_inc(a_full, SLOTS)
            dve.sem_inc(b_kept, SLOTS)

            def stats0(n, c, k):
                dve.wait_ge(loaded[c], k * 32 + 32)
                norm_stats(ln[0], n, c)
                norm_var(ln[0], n, c)

            def row_sums(n, c, k):
                nc.vector.tensor_reduce(S[:, bass.ds(n * NB, NB)], ADJ[c][:], AX.X, ALU.add).then_inc(rowsum, 1)

            def add_bias0(n, c, k):
                dve.wait_ge(l0_out, n + 1)
                dve.wait_ge(beta_added, n + 1)
                nc.vector.tensor_tensor(T1[c][:], bank(c, 0), rows4(B0R), ALU.add).then_inc(l0_biased, 1)

            def residual1(n, c, k):
                dve.wait_ge(l0_biased, n + 1)
                nc.vector.scalar_tensor_tensor(out=chunk(X, n), in0=T1[c][:], scalar=0.0, in1=chunk(X, n),
                                               op0=ALU.max, op1=ALU.add).then_inc(x1_ready, 1)

            def stats1(n, c, k):
                wait_apart(dve, x1_ready, n + 1)
                norm_stats(ln[1], n, c)
                norm_var(ln[1], n, c)

            def scale_shift(L):
                def stage(n, c, k):
                    norm_rstd(L, n, c)
                    norm_shift(L, n, c)
                return stage

            def keep_b(n, c, k):
                dve.wait_ge(ab_ready, n + 1)
                nc.vector.tensor_copy(chunk(BT, n), bank(c, 1)).then_inc(b_kept, 1)

            def full_a(n, c, k):
                dve.wait_ge(a_prod, n + 1)
                nc.vector.tensor_tensor(AF[c][:], bank(c, 0), rows4(B2C), ALU.add).then_inc(a_full, 1)

            def constants():
                dve.wait_ge(weights_in, 16 * WEIGHT_LOADS)
                nc.vector.tensor_reduce(MEANS[:, 0:1], W2[:], AX.X, ALU.add)
                nc.vector.tensor_reduce(MEANS[:, 1:2], B2R[:], AX.X, ALU.add)
                nc.vector.tensor_scalar(NB1[:], B1[:], -1.0, None, ALU.mult)
                nc.vector.tensor_copy(MROW[:], MRAW[:])
                nc.vector.tensor_scalar(E3P1[:], E3[:], 1.0, None, ALU.add).then_inc(setup_step, 1)
                dve.wait_ge(setup_step, 1)
                nc.vector.tensor_scalar(MEANS[:, 2:4], MEANS[:, 0:2], 1.0 / P, None, ALU.mult).then_inc(setup_step, 1)
                dve.wait_ge(setup_step, 2)
                dve.wait_ge(ident_ready, 1)
                nc.vector.tensor_scalar(W2C[:], W2[:], MEANS[:, 2:3], SZ, ALU.subtract, ALU.mult)
                nc.vector.tensor_scalar(NW2C[:], W2[:], MEANS[:, 2:3], -SZ, ALU.subtract, ALU.mult)
                nc.vector.tensor_scalar(B2C[:], B2R[:], MEANS[:, 3:4], SZ, ALU.subtract, ALU.mult)
                nc.vector.tensor_scalar(GAMS[:], GAM[:], 1.0 / (SZ * SW), None, ALU.mult)
                nc.vector.tensor_scalar(DIAGE[:], IDENT[:], E3P1[:, 0:1], None, ALU.mult).then_inc(setup_done, 1)

            def step1(r, q):
                if isinstance(r, int) and (r, q) == (0, 1):
                    constants()
                on(stats1, r, q, 2)
                on(row_sums, r, q, 2)
                on(scale_shift(ln[1]), r, q, 2)
                on(keep_b, r, q, 4)
                on(stats0, r, q, 0)
                on(full_a, r, q, 3)
                on(add_bias0, r, q, 1)
                on(scale_shift(ln[0]), r, q, 0)
                on(residual1, r, q, 1)

            all_steps(dve, step1)

            def hidden(g, k):
                a = NAT[:, bass.ds(g * UG, UG)]
                b = BT[:, bass.ds(graph_of_group(g) * P, P)]
                nc.vector.tensor_tensor(HID[:, slot(k)],
                                        a.rearrange("p (u o) -> p u o", o=1).broadcast_to([P, UG, P]),
                                        b.rearrange("p (o j) -> p o j", o=1).broadcast_to([P, UG, P]),
                                        ALU.max).then_inc(hid_ready, 1)

            def keep_u(g, k):
                wait_apart(dve, ring_free, g + (2 + RING))
                nc.vector.tensor_reduce(NAT[:, bass.ds(g * UG, 2 * UG)],
                                        PS[:, pair_bank(k), 0:4 * UG].rearrange("p (i t) -> p i t", t=2),
                                        AX.X, ALU.add).then_inc(u_free, 1)

            def low_weights(g, k):
                s = slot(k)
                dve.wait_ge(weight_high, g + 1)
                nc.vector.tensor_tensor(W16[:, s, :, 1], W32F[:, s], W16[:, s, :, 0],
                                        ALU.subtract).then_inc(weight_ready, 1)

            def group(g, k, ahead):
                s, z = slot(k), zslot(k)
                dve.wait_ge(act_used, g + 1)
                for u in range(DVE_UNITS):
                    col = (ACT_UNITS + u) % QUAD * P
                    ins = nc.vector.bn_stats(STZ[:, s, u, :], PS[:, 2 * z + 1, col:col + P])
                ins.then_inc(bn_done, 1)
                nc.vector.tensor_tensor(ZL[:, s].rearrange("p u l -> p (u l)"),
                                        PS[:, 2 * z:2 * z + 2, :].rearrange("p a l -> p (a l)"),
                                        ZH[:, s].rearrange("p u l -> p (u l)"), ALU.subtract).then_inc(zl_ready, 1)
                wait_apart(dve, bn_done, g + 1)
                for u in range(DVE_UNITS):
                    ins = nc.vector.bn_aggr(VAR[:, s, ACT_UNITS + u, :], STZ[:, s, u, :])
                ins.then_inc(var_ready, 1)
                if ahead:
                    hidden(g + RING, k + RING)
                if HEAD + k >= 1:
                    low_weights(g - 1, k - 1)
                if k % 2 == 0 and HEAD + k >= 4:
                    keep_u(g - 4, k - 4)

            dve.sem_inc(u_free, 2)
            dve.wait_ge(na_kept, CHUNKS)
            dve.wait_ge(b_kept, CHUNKS + SLOTS)
            dve.wait_ge(a_prod, CHUNKS)
            dve.wait_ge(ab_ready, CHUNKS)
            for g in range(RING):
                hidden(g, g - HEAD)
            dve.wait_ge(a_part2, CHUNKS)
            for k in range(-HEAD, 0):
                group(HEAD + k, k, True)
            with dve.Fori(0, ITERS - 1) as it:
                for k in range(BODY):
                    group(group_at(it, k), k, True)
            for k in range(BODY):
                group(group_at(ITERS - 1, k), k, k + RING < BODY)
            low_weights(GROUPS - 1, BODY - 1)
            keep_u(GROUPS - 4, BODY - 4)
            keep_u(GROUPS - 2, BODY - 2)

            dve.wait_ge(rowsum, CHUNKS)
            nc.vector.tensor_scalar(DINV[:], S[:], 1.0, None, ALU.add).then_inc(deg_ready, 1)
            dve.wait_ge(deg_root, 1)
            nc.vector.reciprocal(DINV[:], DSQ[:]).then_inc(dinv_ready, 1)
            dve.wait_ge(mask_turned, 1)
            nc.vector.tensor_copy(MASK[:], PS[:, 7, 0:GRAPHS]).then_inc(setup_step, 1)
            dve.sem_inc(l3_biased, SLOTS)

            def residual2(n, c, k):
                dve.wait_ge(u_turned, n + 1)
                nc.vector.tensor_tensor(chunk(X, n), chunk(X, n), bank(c, 0), ALU.add).then_inc(x2_ready, 1)

            def stats2(n, c, k):
                wait_apart(dve, x2_ready, n + 1)
                norm_stats(ln[2], n, c)
                norm_var(ln[2], n, c)

            def scale2(n, c, k):
                dve.wait_ge(ln[2].scale, n + 1)
                nc.vector.tensor_tensor(RSD[c][:], RS[c][:], DINV[:, bass.ds(n * NB, NB)], ALU.mult)
                nc.vector.tensor_tensor(NMD[c][:], NM[c][:], DINV[:, bass.ds(n * NB, NB)],
                                        ALU.mult).then_inc(ln[2].scaled, 1)

            def scale_rows(n, c, k):
                dve.wait_ge(l2_out, n + 1)
                nc.vector.tensor_tensor(T1[c][:], bank(c, 0), cols4(DINV, n), ALU.mult).then_inc(l2_normed, 1)

            def residual3(n, c, k):
                dve.wait_ge(l2_normed, n + 1)
                dve.wait_ge(bias_added, n + 1)
                nc.vector.tensor_tensor(chunk(X, n), T1[c][:], chunk(X, n), ALU.add).then_inc(x3_ready, 1)

            def stats3(n, c, k):
                wait_apart(dve, x3_ready, n + 1)
                norm_stats(ln[3], n, c)
                norm_var(ln[3], n, c)

            def add_bias3(n, c, k):
                dve.wait_ge(l3_out, n + 1)
                nc.vector.tensor_tensor(T1[c][:], bank(c, 1), rows4(B32R), ALU.add).then_inc(l3_biased, 1)

            def mask_out(n, c, k):
                dve.wait_ge(l3_biased, n + (1 + SLOTS))
                nc.vector.tensor_tensor(T1[c][:], T1[c][:], cols4(MASK, n), ALU.mult).then_inc(l3_masked, 1)

            def residual4(n, c, k):
                dve.wait_ge(l3_masked, n + 1)
                nc.vector.tensor_tensor(chunk(X, n), T1[c][:], chunk(X, n), ALU.add).then_inc(x4_ready, 1)

            def step3(r, q):
                on(residual3, r, q, 2)
                on(residual2, r, q, 0)
                on(stats3, r, q, 2)
                on(stats2, r, q, 0)
                on(scale_shift(ln[3]), r, q, 2)
                on(add_bias3, r, q, 4)
                on(scale_shift(ln[2]), r, q, 0)
                on(mask_out, r, q, 4)
                on(scale2, r, q, 0)
                on(scale_rows, r, q, 1)
                on(residual4, r, q, 4)

            dve.wait_ge(beta_added, CHUNKS + SLOTS)
            dve.wait_ge(dinv_ready, 1)
            dve.wait_ge(setup_step, 3)
            all_steps(dve, step3)

        @block.tensor
        def _(pe):
            def four(dst, lhs, rhs, *more):
                pairs = [(lhs, rhs), *more]
                for b in range(NB):
                    for k, (l, m) in enumerate(pairs):
                        ins = nc.tensor.matmul(dst[:, b, :], l(b), m(b), start=(k == 0), stop=(k == len(pairs) - 1))
                return ins

            def graph_of(t, n):
                return lambda b: t[:, bass.ds(n * CW + b * P, P)]

            pe.wait_ge(ident_ready, 1)

            def turn_adj(n, c, k):
                pe.wait_ge(loaded[c], k * 32 + 32)
                pe.wait_ge(a_full, n + 1)
                for b in range(NB):
                    ins = nc.tensor.transpose(bank(c, 0)[:, b, :], ADJ[c][:, b, :], IDENT[:])
                ins.then_inc(adj_turned, 1)

            def agg0(n, c, k):
                pe.wait_ge(b_kept, n + 1)
                pe.wait_ge(adjt_kept, n + 1)
                pe.wait_ge(ln[0].h, n + 1)
                four(bank(c, 1), lambda b: H[c][:, b, :], graph_of(ADJT, n)).then_inc(l0_agg, 1)

            def out0(n, c, k):
                pe.wait_ge(l0_agg_copied, n + 1)
                four(bank(c, 0), lambda b: TT[c][:, b, :], lambda b: W0[:]).then_inc(l0_out, 1)

            def turn_h(n, c, k):
                pe.wait_ge(ln[1].h, n + 1)
                for b in range(NB):
                    ins = nc.tensor.transpose(bank(c, 1)[:, b, :], H[c][:, b, :], IDENT[:])
                ins.then_inc(h_turned, 1)

            def a_and_b(n, c, k):
                pe.wait_ge(h_turned_copied, n + 1)
                ht = TT[c][:].rearrange("p b l -> p (b l)")
                nc.tensor.matmul(PS[:, 2 * c, :], W1A[:], ht, start=True, stop=True)
                nc.tensor.matmul(PS[:, 2 * c + 1, :], W1B[:], ht, start=True, stop=True).then_inc(ab_ready, 1)

            def a_times_w2(n, c, k):
                pe.wait_ge(na_kept, n + 1)
                four(bank(c, 0), lambda b: H[c][:, b, :], lambda b: NW2C[:]).then_inc(a_prod, 1)

            def step1(r, q):
                if isinstance(r, int) and (r, q) == (0, 1):
                    pe.wait_ge(setup_done, 1)
                on(turn_adj, r, q, 0)
                on(a_and_b, r, q, 3)
                on(agg0, r, q, 1)
                on(a_times_w2, r, q, 3)
                on(out0, r, q, 1)
                on(turn_h, r, q, 2)

            all_steps(pe, step1)
            pe.wait_ge(b_kept, CHUNKS + SLOTS)
            pe.wait_ge(a_full, CHUNKS + SLOTS)

            def product(g, k, summed=True):
                s, z = slot(k), zslot(k)
                graph = graph_of_group(g)
                pe.wait_ge(rows_in, graph * 16 + 16)
                if not (isinstance(g, int) and g < ZRING):
                    pe.wait_ge(zl_ready, g + (1 - ZRING))
                for q in range(2):
                    nc.tensor.matmul(PS[:, 2 * z + q, :],
                                     SEL[:, bass.ds((g & (GPG - 1)) * 2 + q, 1), :].rearrange("p o j -> p (o j)"),
                                     AROWS[:, bass.ds(graph & 1, 1), :].rearrange("p o l -> p (o l)"),
                                     start=True, stop=False, skip_group_check=True)
                pe.wait_ge(hid_ready, g + 1)
                for u in range(UG):
                    if u == QUAD and summed:
                        weighted_sum(g - RING, k - RING)
                    col = u % QUAD * P
                    ins = nc.tensor.matmul(PS[:, 2 * z + u // QUAD, col:col + P], HID[:, s, u, :], W2C[:],
                                           start=False, stop=(u % QUAD == QUAD - 1), skip_group_check=True)
                ins.then_inc(z_ready, 1)

            def weighted_sum(g, k):
                s = slot(k)
                pe.wait_ge(weight_ready, g + 1)
                pe.wait_ge(zl_ready, g + 1)
                if k % 2 == 0:
                    pe.wait_ge(u_free, (g >> 1) + 1)
                for u in range(UG):
                    col = 2 * (k % 2 * UG + u)
                    nc.tensor.matmul(PS[:, pair_bank(k), col:col + 2], ZH[:, s, u, :], W16[:, s, u, :],
                                     start=True, stop=False, skip_group_check=True)
                    ins = nc.tensor.matmul(PS[:, pair_bank(k), col:col + 1], ZL[:, s, u, :], W16[:, s, u, 0:1],
                                           start=False, stop=True, skip_group_check=True)
                ins.then_inc(ring_free, 1)

            pe.wait_ge(pool_const, 3)
            pe.wait_ge(const_step, 2 + PARTS)
            pe.sem_inc(ring_free, RING)
            for g in range(RING):
                product(g, g - HEAD, summed=False)
            for g in range(RING, HEAD + RING):
                product(g, g - HEAD)
            with pe.Fori(0, ITERS - 1) as it:
                for k in range(RING, BODY + RING):
                    product(group_at(it, k), k)
            for k in range(RING, BODY):
                product(group_at(ITERS - 1, k), k)
            for k in range(BODY - RING, BODY):
                weighted_sum(group_at(ITERS - 1, k), k)

            pe.wait_ge(zl_ready, GROUPS)
            pe.wait_ge(u_free, GROUPS // 2 + 2)
            nc.tensor.transpose(PS[:, 7, 0:GRAPHS], MROW[:], IDENT[0:GRAPHS, 0:GRAPHS]).then_inc(mask_turned, 1)
            pe.wait_ge(setup_step, 3)

            def turn_u(n, c, k):
                pe.wait_ge(u_scaled, n + 1)
                for b in range(NB):
                    ins = nc.tensor.transpose(bank(c, 0)[:, b, :], H[c][:, b, :], IDENT[:])
                ins.then_inc(u_turned, 1)

            def agg2(n, c, k):
                pe.wait_ge(l3_biased, n + 1)
                pe.wait_ge(ln[2].h, n + 1)
                four(bank(c, 1), lambda b: H[c][:, b, :], graph_of(ADJT, n),
                     (lambda b: H[c][:, b, :], lambda b: IDENT[:])).then_inc(l2_agg, 1)

            def out2(n, c, k):
                pe.wait_ge(l2_agg_copied, n + 1)
                four(bank(c, 0), lambda b: TT[c][:, b, :], lambda b: TH[:]).then_inc(l2_out, 1)

            def agg3(n, c, k):
                pe.wait_ge(ln[3].h, n + 1)
                pe.wait_ge(reloaded[c], k * 16 + 16)
                four(bank(c, 1), lambda b: H[c][:, b, :], lambda b: ADJ[c][:, b, :],
                     (lambda b: H[c][:, b, :], lambda b: DIAGE[:])).then_inc(l3_agg, 1)

            def mid3(n, c, k):
                pe.wait_ge(l3_agg_copied, n + 1)
                nc.tensor.matmul(PS[:, 2 * c, :], W31[:], TT[c][:].rearrange("p b l -> p (b l)"),
                                 start=True, stop=True).then_inc(l3_mid, 1)

            def out3(n, c, k):
                pe.wait_ge(l3_relu, n + 1)
                four(bank(c, 1), lambda b: AF[c][:, b, :], lambda b: W32[:]).then_inc(l3_out, 1)

            def step3(r, q):
                on(mid3, r, q, 4)
                on(out2, r, q, 2)
                on(turn_u, r, q, 0)
                on(out3, r, q, 4)
                on(agg3, r, q, 3)
                on(agg2, r, q, 1)

            all_steps(pe, step3)


_ARGS = ["x", "adj", "nodemask", "L0_gnn_W", "L0_gnn_b", "L1_gnn_W1", "L1_gnn_b1", "L1_gnn_W2", "L1_gnn_b2",
         "L1_gnn_gamma", "L1_gnn_beta", "L2_gnn_theta", "L2_gnn_bias", "L3_gnn_W1", "L3_gnn_b1", "L3_gnn_W2",
         "L3_gnn_b2", "L3_gnn_eps"]


def kernel(**inputs):
    import numpy as _np
    import concourse.bacc as _bacc
    from concourse import mybir as _mybir
    from concourse.bass_utils import run_bass_kernel_spmd as _run

    nc = _bacc.Bacc("TRN2", target_bir_lowering=False, num_devices=1)
    arrays, args = {}, []
    for name in _ARGS:
        a = _np.ascontiguousarray(inputs[name])
        if a.dtype == _np.bool_:
            a = a.view(_np.uint8)
        arrays[f"in_{name}"] = a
        args.append(nc.dram_tensor(f"in_{name}", a.shape, _mybir.dt.from_np(a.dtype), kind="ExternalInput").ap())
    out = nc.dram_tensor("out_x", (GRAPHS, P, P), F32, kind="ExternalOutput").ap()
    gnn_stack(nc, *args, out)
    r = _run(nc, [arrays], core_ids=[0])
    return r.results[0]["out_x"]
```
